# Optimizing a Trainium2 kernel written in Bass

```python
import numpy as np
import jax
import jax.numpy as jnp

def _softmax(x, axis=-1):
    return jax.nn.softmax(x, axis=axis)

def _gelu(x):
    return jax.nn.gelu(x, approximate=True)

def _silu(x):
    return jax.nn.silu(x)

def _sigmoid(x):
    return jax.nn.sigmoid(x)

def _layernorm(x, axis=-1, eps=1e-05):
    m = jnp.mean(x, axis=axis, keepdims=True)
    v = jnp.var(x, axis=axis, keepdims=True)
    return (x - m) / jnp.sqrt(v + eps)

def _scatter_add(tgt, idx, src, axis=0):
    return tgt.at[idx].add(src)

def _segment_sum(src, seg, n):
    return jax.ops.segment_sum(src, seg, n)
kernel_name = 'mk_decoder_postln_d2_seqx_r4_540969'

def setup_inputs(seed: int=0):
    np.random.seed(seed)
    _w = jnp.asarray

    def _rec_inputs():
        import jax
        import jax.numpy as jnp
        _rk = jax.random.key(seed)
        x = -0.0002928 + 1 * jax.random.normal(jax.random.fold_in(_rk, 1), (8, 512, 256), jnp.float32)
        _lenS = 512 - jax.random.randint(jax.random.fold_in(_rk, 7), (8,), 0, max(1, 512 // 4) + 1, jnp.int32)
        _lenS2 = 512 - jax.random.randint(jax.random.fold_in(_rk, 8), (8,), 0, max(1, 512 // 4) + 1, jnp.int32)
        _ctx_1024P = jax.random.normal(jax.random.fold_in(_rk, 11), (8, 16, 256), jnp.float32)
        _ctx_1024c = jax.random.dirichlet(jax.random.fold_in(_rk, 511), 0.3 * jnp.ones((16,), jnp.float32), (8, 512))
        _ctx_1024t = jnp.einsum('bsk,bkd->bsd', _ctx_1024c, _ctx_1024P)
        _ctx_1024t = _ctx_1024t * jax.lax.rsqrt(jnp.mean(jnp.square(_ctx_1024t)) + 1e-12) * 0.953939
        ctx_1024 = -1.39393e-06 + 0.999914 * (_ctx_1024t + 0.3 * jax.random.normal(jax.random.fold_in(_rk, 611), (8, 512, 256), jnp.float32))
        return (x, ctx_1024)
    x, ctx_1024 = _rec_inputs()

    def _L0_attn_setup():
        import jax, jax.numpy as jnp
        import numpy as np
        B, T, D = (4, 512, 256)
        H = 4
        K = D
        V = D
        DK = K // H
        DV = V // H
        LOW = 16
        GLN = 16.0

        def _layernorm(x, w, b, eps=1e-05):
            mu = x.mean(-1, keepdims=True)
            xc = x - mu
            var = (xc * xc).mean(-1, keepdims=True)
            return xc * jax.lax.rsqrt(var + eps) * w + b

        def _rmsnorm(x, w, eps=1e-05):
            ms = (x * x).mean(-1, keepdims=True)
            return x * jax.lax.rsqrt(ms + eps) * w

        def _gla_scan(q, k, v, gk):
            scale = DK ** (-0.5)
            qT = jnp.moveaxis(q * scale, 1, 0)
            kT = jnp.moveaxis(k, 1, 0)
            vT = jnp.moveaxis(v, 1, 0)
            gT = jnp.moveaxis(gk, 1, 0)

            def step(h, inp):
                qt, kt, vt, gt = inp
                h = h * jnp.exp(gt)[..., None] + kt[..., :, None] * vt[..., None, :]
                o = jnp.einsum('bhk,bhkv->bhv', qt, h)
                return (h, o)
            h0 = jnp.zeros((q.shape[0], H, DK, DV), q.dtype)
            _, oT = jax.lax.scan(step, h0, (qT, kT, vT, gT))
            return jnp.moveaxis(oT, 0, 1)
        key = jax.random.key(seed)
        ks = jax.random.split(key, 12)
        rn = lambda k, s: jax.random.normal(k, s, jnp.float32) * 0.02
        return {'x': jax.random.normal(ks[0], (B, T, D), jnp.float32), 'ln1_w': jnp.ones((D,), jnp.float32), 'ln1_b': jnp.zeros((D,), jnp.float32), 'Wq': rn(ks[1], (D, K)), 'Wk': rn(ks[2], (D, K)), 'Wv': rn(ks[3], (D, V)), 'Wg': rn(ks[4], (D, V)), 'Wgk1': rn(ks[5], (D, LOW)), 'Wgk2': rn(ks[6], (LOW, K)), 'bgk2': jnp.zeros((K,), jnp.float32), 'rms_w': jnp.ones((DV,), jnp.float32), 'Wo': rn(ks[7], (V, D)), 'ln2_w': jnp.ones((D,), jnp.float32), 'ln2_b': jnp.zeros((D,), jnp.float32), 'W1': rn(ks[8], (D, 3 * D)), 'b1': jnp.zeros((3 * D,), jnp.float32), 'W2': rn(ks[9], (3 * D, D)), 'b2': jnp.zeros((D,), jnp.float32)}
    _L0_attn_all = _L0_attn_setup()
    _L0_attn_in = {k: v for k, v in _L0_attn_all.items() if k in ('ln1_w', 'ln1_b', 'Wq', 'Wk', 'Wv', 'Wg', 'Wgk1', 'Wgk2', 'bgk2', 'rms_w', 'Wo', 'ln2_w', 'ln2_b', 'W1', 'b1', 'W2', 'b2')}
    del _L0_attn_all

    def _L0_xattn_setup():
        import jax, jax.numpy as jnp
        import numpy as np
        B, T, D, H = (2, 512, 256, 16)
        DH = D // H
        key = jax.random.key(seed)
        ks = jax.random.split(key, 11)
        s = 1.0 / np.sqrt(D)
        return {'q': jax.random.normal(ks[0], (B, T, D), jnp.float32), 'k': jax.random.normal(ks[1], (B, T, D), jnp.float32), 'v': jax.random.normal(ks[2], (B, T, D), jnp.float32), 'wq_w': jax.random.normal(ks[3], (D, D), jnp.float32) * s, 'wq_b': jnp.zeros((D,), jnp.float32), 'wk_w': jax.random.normal(ks[4], (D, D), jnp.float32) * s, 'wk_b': jnp.zeros((D,), jnp.float32), 'wv_w': jax.random.normal(ks[5], (D, D), jnp.float32) * s, 'wv_b': jnp.zeros((D,), jnp.float32), 'wo_w': jax.random.normal(ks[6], (D, D), jnp.float32) * s, 'wo_b': jnp.zeros((D,), jnp.float32)}
    _L0_xattn_all = _L0_xattn_setup()
    _L0_xattn_in = {k: v for k, v in _L0_xattn_all.items() if k in ('wq_w', 'wq_b', 'wk_w', 'wk_b', 'wv_w', 'wv_b', 'wo_w', 'wo_b')}
    del _L0_xattn_all

    def _L0_ffn_setup():
        import jax, jax.numpy as jnp
        import numpy as np
        B, S, H = (2, 512, 256)
        E_DYN, E_FIX = (8, 1)
        I_DYN, I_FIX = (128, 512)
        TOP_K = 4
        TOP_P = 0.75
        JITTER_EPS = 0.1
        CAPACITY_FACTOR = 1.25
        MIN_CAPACITY = 4

        def _sparse_mixer(scores):
            T = scores.shape[0]
            rows = jnp.arange(T)
            masked_scores = scores
            mults, sels = ([], [])
            for _ in range(TOP_K):
                thr = jnp.max(masked_scores, axis=-1, keepdims=True)
                sel = jnp.argmax(masked_scores, axis=-1)
                factor = jnp.maximum(jnp.abs(scores), jnp.abs(thr))
                jmask = (thr - scores) / factor > 2.0 * JITTER_EPS
                gates = jax.nn.softmax(jnp.where(jmask, -jnp.inf, masked_scores), axis=-1)
                mult = jnp.take_along_axis(gates, sel[:, None], axis=-1)[:, 0]
                masked_scores = masked_scores.at[rows, sel].set(-jnp.inf)
                mults.append(mult)
                sels.append(sel)
            return (jnp.stack(mults, axis=-1), jnp.stack(sels, axis=-1))
        key = jax.random.key(seed)
        k = jax.random.split(key, 8)
        sc = 0.02
        return {'hidden_states': jax.random.normal(k[0], (B, S, H), jnp.float32), 'gate_w': jax.random.normal(k[1], (E_DYN + E_FIX, H), jnp.float32) * sc, 'dyn_gate_w': jax.random.normal(k[2], (E_DYN, I_DYN, H), jnp.float32) * sc, 'dyn_up_w': jax.random.normal(k[3], (E_DYN, I_DYN, H), jnp.float32) * sc, 'dyn_down_w': jax.random.normal(k[4], (E_DYN, H, I_DYN), jnp.float32) * sc, 'sh_gate_w': jax.random.normal(k[5], (E_FIX, I_FIX, H), jnp.float32) * sc, 'sh_up_w': jax.random.normal(k[6], (E_FIX, I_FIX, H), jnp.float32) * sc, 'sh_down_w': jax.random.normal(k[7], (E_FIX, H, I_FIX), jnp.float32) * sc}
    _L0_ffn_all = _L0_ffn_setup()
    _L0_ffn_in = {k: v for k, v in _L0_ffn_all.items() if k in ('gate_w', 'dyn_gate_w', 'dyn_up_w', 'dyn_down_w', 'sh_gate_w', 'sh_up_w', 'sh_down_w')}
    del _L0_ffn_all

    def _L1_attn_setup():
        import jax, jax.numpy as jnp
        import numpy as np
        D_MODEL = 256
        D_STATE = 128
        HEAD_DIM = 64
        EXPAND = 2
        K = 4
        N_GROUPS = 1
        D_INNER = EXPAND * D_MODEL
        N_HEADS = D_INNER // HEAD_DIM
        D_PROJ = 2 * D_INNER + 2 * N_GROUPS * D_STATE + N_HEADS
        EPS = 1e-06

        def _rmsnorm(x, w):
            return x * jax.lax.rsqrt(jnp.mean(x * x, axis=-1, keepdims=True) + EPS) * w
        key = jax.random.key(seed)
        ks = jax.random.split(key, 8)
        B, L = (2, 512)
        x = jax.random.normal(ks[0], (B, L, D_MODEL), jnp.float32)
        norm_w = jnp.ones((D_MODEL,), jnp.float32)
        in_proj_w = jax.random.normal(ks[1], (D_PROJ, D_MODEL), jnp.float32) / np.sqrt(D_MODEL).astype(np.float32)
        conv_w = jax.random.normal(ks[2], (D_INNER, K), jnp.float32) / np.sqrt(K).astype(np.float32)
        conv_b = jnp.zeros((D_INNER,), jnp.float32)
        A_log = jnp.log(jax.random.uniform(ks[3], (N_HEADS,), jnp.float32) * 15.0 + 1.0)
        D = jnp.ones((N_HEADS,), jnp.float32)
        dt_bias = jnp.log(jax.random.uniform(ks[4], (N_HEADS,), jnp.float32) * 0.099 + 0.001)
        out_proj_w = jax.random.normal(ks[5], (D_MODEL, D_INNER), jnp.float32) / np.sqrt(D_INNER).astype(np.float32)
        return dict(x=x, norm_w=norm_w, in_proj_w=in_proj_w, conv_w=conv_w, conv_b=conv_b, A_log=A_log, D=D, dt_bias=dt_bias, out_proj_w=out_proj_w)
    _L1_attn_all = _L1_attn_setup()
    _L1_attn_in = {k: v for k, v in _L1_attn_all.items() if k in ('norm_w', 'in_proj_w', 'conv_w', 'conv_b', 'A_log', 'D', 'dt_bias', 'out_proj_w')}
    del _L1_attn_all

    def _L1_xattn_setup():
        import jax, jax.numpy as jnp
        import numpy as np
        B, S, D, H = (2, 512, 256, 4)
        DK = D // H

        def _psi(x, proj_w, proj_b):
            gen = x @ proj_w.T + proj_b
            A, Bg = (gen[..., 0:8], gen[..., 8:16])
            Th = jnp.clip(gen[..., 16:24], -8.0, 8.0)
            psi_real = A * jnp.exp(Th) + Bg * jnp.cos(Th)
            psi_imag = Bg * jnp.sin(Th)
            return jnp.concatenate([psi_real, psi_imag], axis=-1)
        key = jax.random.key(seed)
        ks = jax.random.split(key, 12)
        inp = {'Q_input': jax.random.normal(ks[0], (B, S, D), jnp.float32), 'K': jax.random.normal(ks[1], (B, S, D), jnp.float32), 'V': jax.random.normal(ks[2], (B, S, D), jnp.float32), 'T_field': jax.random.normal(ks[3], (32, 32, 16, 16), jnp.float32), 'Wq_w': jax.random.normal(ks[4], (D, D), jnp.float32) * 0.02, 'Wq_b': jnp.zeros((D,), jnp.float32), 'Wo_w': jax.random.normal(ks[5], (D, D), jnp.float32) * 0.02, 'Wo_b': jnp.zeros((D,), jnp.float32), 'proj_w': jax.random.normal(ks[6], (24, DK), jnp.float32) * 0.02, 'proj_b': jnp.zeros((24,), jnp.float32), 'geo_w': jnp.ones((4,), jnp.float32), 'temperature': jnp.asarray(1.0, jnp.float32)}
        return inp
    _L1_xattn_all = _L1_xattn_setup()
    _L1_xattn_in = {k: v for k, v in _L1_xattn_all.items() if k in ('T_field', 'Wq_w', 'Wq_b', 'Wo_w', 'Wo_b', 'proj_w', 'proj_b', 'geo_w', 'temperature')}
    del _L1_xattn_all

    def _L1_ffn_setup():
        import jax, jax.numpy as jnp
        import numpy as np
        DIM = 256
        HIDDEN = 768
        SCALE = 1.0 / 127.0

        def _dequant(w_int, dtype):
            return w_int.astype(dtype) * jnp.asarray(SCALE, dtype)
        key = jax.random.key(seed)
        k_x, k_g, k_u, k_d = jax.random.split(key, 4)
        x = jax.random.normal(k_x, (4, 512, DIM), dtype=jnp.float32)
        w_gate = jax.random.randint(k_g, (HIDDEN, DIM), -127, 128, dtype=jnp.int32)
        w_up = jax.random.randint(k_u, (HIDDEN, DIM), -127, 128, dtype=jnp.int32)
        w_down = jax.random.randint(k_d, (DIM, HIDDEN), -127, 128, dtype=jnp.int32)
        return {'x': x, 'w_gate': w_gate, 'w_up': w_up, 'w_down': w_down}
    _L1_ffn_all = _L1_ffn_setup()
    _L1_ffn_in = {k: v for k, v in _L1_ffn_all.items() if k in ('w_gate', 'w_up', 'w_down')}
    del _L1_ffn_all
    return {'x': x, 'ctx_1024': ctx_1024, 'L0_attn_ln1_w': _L0_attn_in['ln1_w'], 'L0_attn_ln1_b': _L0_attn_in['ln1_b'], 'L0_attn_Wq': _L0_attn_in['Wq'], 'L0_attn_Wk': _L0_attn_in['Wk'], 'L0_attn_Wv': _L0_attn_in['Wv'], 'L0_attn_Wg': _L0_attn_in['Wg'], 'L0_attn_Wgk1': _L0_attn_in['Wgk1'], 'L0_attn_Wgk2': _L0_attn_in['Wgk2'], 'L0_attn_bgk2': _L0_attn_in['bgk2'], 'L0_attn_rms_w': _L0_attn_in['rms_w'], 'L0_attn_Wo': _L0_attn_in['Wo'], 'L0_attn_ln2_w': _L0_attn_in['ln2_w'], 'L0_attn_ln2_b': _L0_attn_in['ln2_b'], 'L0_attn_W1': _L0_attn_in['W1'], 'L0_attn_b1': _L0_attn_in['b1'], 'L0_attn_W2': _L0_attn_in['W2'], 'L0_attn_b2': _L0_attn_in['b2'], 'L0_xattn_wq_w': _L0_xattn_in['wq_w'], 'L0_xattn_wq_b': _L0_xattn_in['wq_b'], 'L0_xattn_wk_w': _L0_xattn_in['wk_w'], 'L0_xattn_wk_b': _L0_xattn_in['wk_b'], 'L0_xattn_wv_w': _L0_xattn_in['wv_w'], 'L0_xattn_wv_b': _L0_xattn_in['wv_b'], 'L0_xattn_wo_w': _L0_xattn_in['wo_w'], 'L0_xattn_wo_b': _L0_xattn_in['wo_b'], 'L0_ffn_gate_w': _L0_ffn_in['gate_w'], 'L0_ffn_dyn_gate_w': _L0_ffn_in['dyn_gate_w'], 'L0_ffn_dyn_up_w': _L0_ffn_in['dyn_up_w'], 'L0_ffn_dyn_down_w': _L0_ffn_in['dyn_down_w'], 'L0_ffn_sh_gate_w': _L0_ffn_in['sh_gate_w'], 'L0_ffn_sh_up_w': _L0_ffn_in['sh_up_w'], 'L0_ffn_sh_down_w': _L0_ffn_in['sh_down_w'], 'L1_attn_norm_w': _L1_attn_in['norm_w'], 'L1_attn_in_proj_w': _L1_attn_in['in_proj_w'], 'L1_attn_conv_w': _L1_attn_in['conv_w'], 'L1_attn_conv_b': _L1_attn_in['conv_b'], 'L1_attn_A_log': _L1_attn_in['A_log'], 'L1_attn_D': _L1_attn_in['D'], 'L1_attn_dt_bias': _L1_attn_in['dt_bias'], 'L1_attn_out_proj_w': _L1_attn_in['out_proj_w'], 'L1_xattn_T_field': _L1_xattn_in['T_field'], 'L1_xattn_Wq_w': _L1_xattn_in['Wq_w'], 'L1_xattn_Wq_b': _L1_xattn_in['Wq_b'], 'L1_xattn_Wo_w': _L1_xattn_in['Wo_w'], 'L1_xattn_Wo_b': _L1_xattn_in['Wo_b'], 'L1_xattn_proj_w': _L1_xattn_in['proj_w'], 'L1_xattn_proj_b': _L1_xattn_in['proj_b'], 'L1_xattn_geo_w': _L1_xattn_in['geo_w'], 'L1_xattn_temperature': _L1_xattn_in['temperature'], 'L1_ffn_w_gate': _L1_ffn_in['w_gate'], 'L1_ffn_w_up': _L1_ffn_in['w_up'], 'L1_ffn_w_down': _L1_ffn_in['w_down']}

def reference(x, ctx_1024, L0_attn_ln1_w, L0_attn_ln1_b, L0_attn_Wq, L0_attn_Wk, L0_attn_Wv, L0_attn_Wg, L0_attn_Wgk1, L0_attn_Wgk2, L0_attn_bgk2, L0_attn_rms_w, L0_attn_Wo, L0_attn_ln2_w, L0_attn_ln2_b, L0_attn_W1, L0_attn_b1, L0_attn_W2, L0_attn_b2, L0_xattn_wq_w, L0_xattn_wq_b, L0_xattn_wk_w, L0_xattn_wk_b, L0_xattn_wv_w, L0_xattn_wv_b, L0_xattn_wo_w, L0_xattn_wo_b, L0_ffn_gate_w, L0_ffn_dyn_gate_w, L0_ffn_dyn_up_w, L0_ffn_dyn_down_w, L0_ffn_sh_gate_w, L0_ffn_sh_up_w, L0_ffn_sh_down_w, L1_attn_norm_w, L1_attn_in_proj_w, L1_attn_conv_w, L1_attn_conv_b, L1_attn_A_log, L1_attn_D, L1_attn_dt_bias, L1_attn_out_proj_w, L1_xattn_T_field, L1_xattn_Wq_w, L1_xattn_Wq_b, L1_xattn_Wo_w, L1_xattn_Wo_b, L1_xattn_proj_w, L1_xattn_proj_b, L1_xattn_geo_w, L1_xattn_temperature, L1_ffn_w_gate, L1_ffn_w_up, L1_ffn_w_down):
    import jax
    import jax.numpy as jnp

    def _L0_attn_ref(x, ln1_w, ln1_b, Wq, Wk, Wv, Wg, Wgk1, Wgk2, bgk2, rms_w, Wo, ln2_w, ln2_b, W1, b1, W2, b2):
        import jax, jax.numpy as jnp
        import numpy as np
        B, T, D = (4, 512, 256)
        H = 4
        K = D
        V = D
        DK = K // H
        DV = V // H
        LOW = 16
        GLN = 16.0

        def _layernorm(x, w, b, eps=1e-05):
            mu = x.mean(-1, keepdims=True)
            xc = x - mu
            var = (xc * xc).mean(-1, keepdims=True)
            return xc * jax.lax.rsqrt(var + eps) * w + b

        def _rmsnorm(x, w, eps=1e-05):
            ms = (x * x).mean(-1, keepdims=True)
            return x * jax.lax.rsqrt(ms + eps) * w

        def _gla_scan(q, k, v, gk):
            scale = DK ** (-0.5)
            qT = jnp.moveaxis(q * scale, 1, 0)
            kT = jnp.moveaxis(k, 1, 0)
            vT = jnp.moveaxis(v, 1, 0)
            gT = jnp.moveaxis(gk, 1, 0)

            def step(h, inp):
                qt, kt, vt, gt = inp
                h = h * jnp.exp(gt)[..., None] + kt[..., :, None] * vt[..., None, :]
                o = jnp.einsum('bhk,bhkv->bhv', qt, h)
                return (h, o)
            h0 = jnp.zeros((q.shape[0], H, DK, DV), q.dtype)
            _, oT = jax.lax.scan(step, h0, (qT, kT, vT, gT))
            return jnp.moveaxis(oT, 0, 1)
        b, t = (x.shape[0], x.shape[1])
        xn = _layernorm(x, ln1_w, ln1_b)
        q = (xn @ Wq).reshape(b, t, H, DK)
        k = (xn @ Wk).reshape(b, t, H, DK)
        v = (xn @ Wv).reshape(b, t, H, DV)
        gk = (jax.nn.log_sigmoid(xn @ Wgk1 @ Wgk2 + bgk2) / GLN).reshape(b, t, H, DK)
        o = _gla_scan(q, k, v, gk)
        g = (xn @ Wg).reshape(b, t, H, DV)
        o = _rmsnorm(o, rms_w) * (g * jax.nn.sigmoid(g))
        o = o.reshape(b, t, V) @ Wo
        x = x + o
        xn2 = _layernorm(x, ln2_w, ln2_b)
        h = jax.nn.leaky_relu(xn2 @ W1 + b1, 0.01)
        h = h * h
        x = x + (h @ W2 + b2)
        return x

    def _L0_xattn_ref(q, k, v, wq_w, wq_b, wk_w, wk_b, wv_w, wv_b, wo_w, wo_b):
        import jax, jax.numpy as jnp
        import numpy as np
        B, T, D, H = (2, 512, 256, 16)
        DH = D // H
        b, t, d = q.shape
        wq = (q @ wq_w.T + wq_b).reshape(b, t, H, DH)
        wk = (k @ wk_w.T + wk_b).reshape(b, t, H, DH)
        wv = (v @ wv_w.T + wv_b).reshape(b, t, H, DH)
        scores = jnp.einsum('bthd,bshd->bhts', wq, wk) / jnp.sqrt(jnp.float32(DH))
        probs = jax.nn.softmax(scores, axis=-1)
        attn = jnp.einsum('bhts,bshd->bthd', probs, wv)
        attn = attn.reshape(b, t, d)
        return attn @ wo_w.T + wo_b

    def _L0_ffn_ref(hidden_states, gate_w, dyn_gate_w, dyn_up_w, dyn_down_w, sh_gate_w, sh_up_w, sh_down_w):
        import jax, jax.numpy as jnp
        import numpy as np
        B, S, H = (2, 512, 256)
        E_DYN, E_FIX = (8, 1)
        I_DYN, I_FIX = (128, 512)
        TOP_K = 4
        TOP_P = 0.75
        JITTER_EPS = 0.1
        CAPACITY_FACTOR = 1.25
        MIN_CAPACITY = 4

        def _sparse_mixer(scores):
            T = scores.shape[0]
            rows = jnp.arange(T)
            masked_scores = scores
            mults, sels = ([], [])
            for _ in range(TOP_K):
                thr = jnp.max(masked_scores, axis=-1, keepdims=True)
                sel = jnp.argmax(masked_scores, axis=-1)
                factor = jnp.maximum(jnp.abs(scores), jnp.abs(thr))
                jmask = (thr - scores) / factor > 2.0 * JITTER_EPS
                gates = jax.nn.softmax(jnp.where(jmask, -jnp.inf, masked_scores), axis=-1)
                mult = jnp.take_along_axis(gates, sel[:, None], axis=-1)[:, 0]
                masked_scores = masked_scores.at[rows, sel].set(-jnp.inf)
                mults.append(mult)
                sels.append(sel)
            return (jnp.stack(mults, axis=-1), jnp.stack(sels, axis=-1))
        Bv, Sv, Hv = hidden_states.shape
        T = Bv * Sv
        x = hidden_states.reshape(T, Hv)
        full_logits = x @ gate_w.T
        dyn_logits = full_logits[:, :E_DYN]
        probs = jax.nn.softmax(dyn_logits, axis=-1)
        sorted_p = jnp.sort(probs, axis=-1)[:, ::-1]
        csum = jnp.cumsum(sorted_p, axis=-1)
        dyn_k = jnp.minimum(jnp.sum(csum < TOP_P, axis=-1) + 1, TOP_K)
        mult, sel = _sparse_mixer(dyn_logits)
        slot_valid = jnp.arange(TOP_K)[None, :] < dyn_k[:, None]
        mult = jnp.where(slot_valid, mult, 0.0)
        rows = jnp.arange(T)
        rw = jnp.zeros((T, E_DYN), x.dtype).at[rows[:, None], sel].add(mult)
        rw = rw / jnp.sum(rw, axis=-1, keepdims=True)
        mask_dyn = (rw > 0).astype(jnp.int32)
        cap = max(int(np.ceil(T / E_DYN * CAPACITY_FACTOR)), MIN_CAPACITY)
        mask_dyn = mask_dyn * (jnp.cumsum(mask_dyn, axis=0) <= cap)
        expert_mask = jnp.concatenate([mask_dyn, jnp.ones((T, E_FIX), jnp.int32)], axis=-1)
        maskf = expert_mask.astype(x.dtype)
        gw = jax.nn.softmax(jnp.where(expert_mask == 0, -jnp.inf, full_logits), axis=-1)
        gd = rw * jnp.sum(gw[:, :E_DYN], axis=-1, keepdims=True)
        global_w = jnp.concatenate([gd, gw[:, E_DYN:]], axis=-1) * maskf
        g = jnp.einsum('th,eih->tei', x, dyn_gate_w)
        u = jnp.einsum('th,eih->tei', x, dyn_up_w)
        y_dyn = jnp.einsum('tei,ehi->teh', jax.nn.silu(g) * u, dyn_down_w)
        out = jnp.einsum('te,teh->th', global_w[:, :E_DYN], y_dyn)
        gs = jnp.einsum('th,fih->tfi', x, sh_gate_w)
        us = jnp.einsum('th,fih->tfi', x, sh_up_w)
        y_sh = jnp.einsum('tfi,fhi->tfh', jax.nn.silu(gs) * us, sh_down_w)
        out = out + jnp.einsum('tf,tfh->th', global_w[:, E_DYN:], y_sh)
        return out.reshape(Bv, Sv, Hv)

    def _L1_attn_ref(x, norm_w, in_proj_w, conv_w, conv_b, A_log, D, dt_bias, out_proj_w):
        import jax, jax.numpy as jnp
        import numpy as np
        D_MODEL = 256
        D_STATE = 128
        HEAD_DIM = 64
        EXPAND = 2
        K = 4
        N_GROUPS = 1
        D_INNER = EXPAND * D_MODEL
        N_HEADS = D_INNER // HEAD_DIM
        D_PROJ = 2 * D_INNER + 2 * N_GROUPS * D_STATE + N_HEADS
        EPS = 1e-06

        def _rmsnorm(x, w):
            return x * jax.lax.rsqrt(jnp.mean(x * x, axis=-1, keepdims=True) + EPS) * w
        batch, L, _ = x.shape
        residual = x
        xn = _rmsnorm(x, norm_w)
        proj = jnp.einsum('bld,pd->blp', xn, in_proj_w)
        i = 0
        z = proj[:, :, i:i + D_INNER]
        i += D_INNER
        x_ssm = proj[:, :, i:i + D_INNER]
        i += D_INNER
        bc = N_GROUPS * D_STATE
        Bm = proj[:, :, i:i + bc].reshape(batch, L, N_GROUPS, D_STATE)
        i += bc
        Cm = proj[:, :, i:i + bc].reshape(batch, L, N_GROUPS, D_STATE)
        i += bc
        dt_raw = proj[:, :, i:i + N_HEADS]
        xp = jnp.pad(x_ssm, ((0, 0), (K - 1, 0), (0, 0)))
        x_conv = conv_b
        for k in range(K):
            x_conv = x_conv + xp[:, k:k + L, :] * conv_w[:, k]
        x_conv = jax.nn.silu(x_conv)
        xh = x_conv.reshape(batch, L, N_HEADS, HEAD_DIM)
        dt = jax.nn.softplus(dt_raw + dt_bias)
        dA = jnp.exp(-jnp.exp(A_log) * dt)
        dtx = dt[..., None] * xh
        gidx = jnp.arange(N_HEADS) // (N_HEADS // N_GROUPS)
        Bg = Bm[:, :, gidx, :]
        Cg = Cm[:, :, gidx, :]

        def step(h, inp):
            dA_t, dtx_t, B_t, C_t = inp
            h = h * dA_t[:, :, None, None] + dtx_t[..., None] * B_t[:, :, None, :]
            y_t = jnp.einsum('bhpn,bhn->bhp', h, C_t)
            return (h, y_t)
        h0 = jnp.zeros((batch, N_HEADS, HEAD_DIM, D_STATE), jnp.float32)
        xs = (jnp.swapaxes(dA, 0, 1), jnp.swapaxes(dtx, 0, 1), jnp.swapaxes(Bg, 0, 1), jnp.swapaxes(Cg, 0, 1))
        _, ys = jax.lax.scan(step, h0, xs)
        y = jnp.swapaxes(ys, 0, 1) + D[None, None, :, None] * xh
        y = y.reshape(batch, L, D_INNER) * jax.nn.silu(z)
        return residual + jnp.einsum('bli,di->bld', y, out_proj_w)

    def _L1_xattn_ref(Q_input, K, V, T_field, Wq_w, Wq_b, Wo_w, Wo_b, proj_w, proj_b, geo_w, temperature):
        import jax, jax.numpy as jnp
        import numpy as np
        B, S, D, H = (2, 512, 256, 4)
        DK = D // H

        def _psi(x, proj_w, proj_b):
            gen = x @ proj_w.T + proj_b
            A, Bg = (gen[..., 0:8], gen[..., 8:16])
            Th = jnp.clip(gen[..., 16:24], -8.0, 8.0)
            psi_real = A * jnp.exp(Th) + Bg * jnp.cos(Th)
            psi_imag = Bg * jnp.sin(Th)
            return jnp.concatenate([psi_real, psi_imag], axis=-1)
        b, sq, d = Q_input.shape
        sk = K.shape[1]
        dk = d // H
        Q = (Q_input @ Wq_w.T + Wq_b).reshape(b, sq, H, dk).transpose(0, 2, 1, 3)
        Kh = K.reshape(b, sk, H, dk).transpose(0, 2, 1, 3)
        Vh = V.reshape(b, sk, H, dk).transpose(0, 2, 1, 3)
        pq = _psi(Q, proj_w, proj_b)
        pk = _psi(Kh, proj_w, proj_b)
        qr, qi = (pq[..., :8], pq[..., 8:])
        kr, ki = (pk[..., :8], pk[..., 8:])
        tensor = jnp.einsum('bhqd,bhkd->bhqk', qr, kr) + jnp.einsum('bhqd,bhkd->bhqk', qi, ki)
        spinor = jnp.einsum('bhqd,bhkd->bhqk', qr, ki) - jnp.einsum('bhqd,bhkd->bhqk', qi, kr)
        qn2 = jnp.sum(pq * pq, -1)
        kn2 = jnp.sum(pk * pk, -1)
        gram = qn2[..., :, None] * kn2[..., None, :]
        wedge = jnp.sqrt(jnp.maximum(gram - tensor ** 2 - spinor ** 2, 0.0) + 1e-06)
        hodge = jnp.sqrt(qn2 + 1e-06)[..., :, None] * jnp.sqrt(kn2 + 1e-06)[..., None, :]
        scores = (geo_w[0] * wedge + geo_w[1] * tensor + geo_w[2] * spinor + geo_w[3] * hodge) / 4.0
        scores = scores / temperature
        w = jax.nn.softmax(scores, axis=-1)
        out = jnp.einsum('bhqk,bhkd->bhqd', w, Vh)
        out = out.transpose(0, 2, 1, 3).reshape(b, sq, d)
        return out @ Wo_w.T + Wo_b

    def _L1_ffn_ref(x, w_gate, w_up, w_down):
        import jax, jax.numpy as jnp
        import numpy as np
        DIM = 256
        HIDDEN = 768
        SCALE = 1.0 / 127.0

        def _dequant(w_int, dtype):
            return w_int.astype(dtype) * jnp.asarray(SCALE, dtype)
        wg = _dequant(w_gate, x.dtype)
        wu = _dequant(w_up, x.dtype)
        wd = _dequant(w_down, x.dtype)
        gate = jnp.einsum('bsd,hd->bsh', x, wg)
        up = jnp.einsum('bsd,hd->bsh', x, wu)
        h = jax.nn.silu(gate) * up
        return jnp.einsum('bsh,dh->bsd', h, wd)
    x = _layernorm(x + _L0_attn_ref(x, L0_attn_ln1_w, L0_attn_ln1_b, L0_attn_Wq, L0_attn_Wk, L0_attn_Wv, L0_attn_Wg, L0_attn_Wgk1, L0_attn_Wgk2, L0_attn_bgk2, L0_attn_rms_w, L0_attn_Wo, L0_attn_ln2_w, L0_attn_ln2_b, L0_attn_W1, L0_attn_b1, L0_attn_W2, L0_attn_b2), axis=-1)
    x = _layernorm(x + _L0_xattn_ref(x, ctx_1024, ctx_1024, L0_xattn_wq_w, L0_xattn_wq_b, L0_xattn_wk_w, L0_xattn_wk_b, L0_xattn_wv_w, L0_xattn_wv_b, L0_xattn_wo_w, L0_xattn_wo_b), axis=-1)
    x = _layernorm(x + _L0_ffn_ref(x, L0_ffn_gate_w, L0_ffn_dyn_gate_w, L0_ffn_dyn_up_w, L0_ffn_dyn_down_w, L0_ffn_sh_gate_w, L0_ffn_sh_up_w, L0_ffn_sh_down_w), axis=-1)
    x = _layernorm(x + _L1_attn_ref(x, L1_attn_norm_w, L1_attn_in_proj_w, L1_attn_conv_w, L1_attn_conv_b, L1_attn_A_log, L1_attn_D, L1_attn_dt_bias, L1_attn_out_proj_w), axis=-1)
    x = _layernorm(x + _L1_xattn_ref(x, ctx_1024, ctx_1024, L1_xattn_T_field, L1_xattn_Wq_w, L1_xattn_Wq_b, L1_xattn_Wo_w, L1_xattn_Wo_b, L1_xattn_proj_w, L1_xattn_proj_b, L1_xattn_geo_w, L1_xattn_temperature), axis=-1)
    x = _layernorm(x + _L1_ffn_ref(x, L1_ffn_w_gate, L1_ffn_w_up, L1_ffn_w_down), axis=-1)
    return x

_drawn_inputs = setup_inputs


def setup_inputs(seed=0):
    import zlib

    import numpy as np

    out = dict(_drawn_inputs(seed))
    spreads = {'L0_attn_ln1_w': (1.0, 0.6),
     'L0_attn_ln1_b': (0.0, 0.8),
     'L0_attn_bgk2': (0.0, 0.8),
     'L0_attn_rms_w': (1.0, 0.6),
     'L0_attn_ln2_w': (1.0, 0.6),
     'L0_attn_ln2_b': (0.0, 0.8),
     'L0_attn_b1': (0.0, 0.372),
     'L0_attn_b2': (0.0, 0.1),
     'L0_xattn_wq_b': (0.0, 0.1),
     'L0_xattn_wk_b': (0.0, 0.8),
     'L0_xattn_wv_b': (0.0, 0.1),
     'L0_xattn_wo_b': (0.0, 0.1),
     'L1_attn_norm_w': (1.0, 0.2),
     'L1_attn_conv_b': (0.0, 0.1),
     'L1_attn_D': (1.0, 0.2),
     'L1_xattn_Wq_b': (0.0, 0.8),
     'L1_xattn_Wo_b': (0.0, 0.1),
     'L1_xattn_proj_b': (0.0, 0.8),
     'L1_xattn_geo_w': (1.0, 0.6)}
    factors = {'L0_attn_Wgk1': 8.0,
     'L0_attn_Wgk2': 8.0,
     'L0_ffn_gate_w': 8.0,
     'L0_ffn_dyn_gate_w': 8.0,
     'L0_ffn_dyn_up_w': 8.0,
     'L0_ffn_dyn_down_w': 8.0,
     'L1_xattn_Wq_w': 8.0,
     'L1_xattn_proj_w': 8.0}
    for name, (base, spread) in spreads.items():
        noise = np.random.default_rng([zlib.crc32(name.encode()), seed]).standard_normal(out[name].shape)
        drawn = base * np.exp(spread * noise) if base else spread * noise
        out[name] = jnp.asarray(drawn.astype(out[name].dtype))
    for name, factor in factors.items():
        out[name] = (out[name] * factor).astype(out[name].dtype)
    return out
```

```python
from contextlib import ExitStack

import concourse.bass as bass
from concourse import mybir

F32 = mybir.dt.float32
F32R = mybir.dt.float32r
I32 = mybir.dt.int32
U32 = mybir.dt.uint32
ALU = mybir.AluOpType
ACT = mybir.ActivationFunctionType
AX = mybir.AxisListType.X
PI = 3.141592653589793
TURN_HI = 6.28125
TURN_LO = 2 * PI - TURN_HI
ROUND = 12582912.0

P = 128
B, T, D = 8, 512, 256
NT = T // P
DC = D // P
GH = 4
XH = 16
XQ = XH // 4
NE, TOPK, CAP, TOP_P, JITTER = 8, 4, 640, 0.75, 0.1
SHF = 4
MH, MN = 8, 128
MF = 4
SUB = 32
NSUB = P // SUB
HID = 768
HF = HID // P
LIN = 96
LOW = 16
REGIONS, LONG = 3, 3


def f3(v, c):
    return v.rearrange("p (c n) -> p c n", c=c)


def flat(v):
    return v.rearrange("p a n -> p (a n)")


def over(v, n):
    return v.unsqueeze(2).to_broadcast([v.shape[0], v.shape[1], n])


def times(v, n):
    return v.unsqueeze(1).to_broadcast([v.shape[0], n, v.shape[1]])


def counter():
    return iter(range(1, 1 << 20)).__next__


class Stage:

    def __init__(self, nc, ctx, label, psum, sems):
        self.nc, self.ctx, self.label, self.psum = nc, ctx, label, psum
        self.sems, self.place, self.uses, self.short = sems, {}, [0] * (REGIONS + 1), 0

    def sb(self, name, shape, dt=F32):
        return self.ctx.enter_context(self.nc.sbuf_tensor(f"{self.label}_{name}", [P] + shape, dt))

    def sem(self, name):
        if name not in self.sems:
            self.sems[name] = self.sems["keep"].enter_context(self.nc.semaphore(name))
        return self.sems[name]

    def claim(self, name, long=False):
        r = LONG if long else self.short % REGIONS
        self.short += not long
        n = self.uses[r]
        self.uses[r] += 1
        self.place[name] = (r, n)
        if n:
            self.nc.tensor.wait_ge(self.sem(f"psum_free{r}"), n)
        return self.psum[r]

    def region(self, name):
        return self.psum[self.place[name][0]]

    def filling(self, name):
        return self.sem(f"psum_full{self.place[name][0]}")

    def emptying(self, name):
        return self.sem(f"psum_free{self.place[name][0]}")

    def full(self, name):
        return self.filling(name), self.place[name][1] + 1

    def emptied(self, name):
        return self.emptying(name), self.place[name][1] + 1

    def zero_sems(self):
        nums = sorted(s.num for n, s in self.sems.items() if n != "keep")
        assert nums == list(range(nums[0], nums[-1] + 1)), nums
        self.nc.multi_engine_barrier(list(self.nc.engines), sems_to_clear=range(nums[0], nums[-1] + 1))


def transposes(st, pe, name, src, ident):
    o = st.claim(name)
    for c in range(DC):
        for t in range(NT):
            last = st.nc.tensor.transpose(o[:, c, t * P:t * P + P], src[:, t, c * P:c * P + P], ident)
    last.then_inc(st.filling(name), 1)


def feature_major(st, name, w, col, rhs, tiles=2, m=P, kc=DC):
    o = st.claim(name)
    for i in range(tiles):
        for c in range(kc):
            last = st.nc.tensor.matmul(o[0:m, i, :], w[:, c, col + i * P:col + i * P + m], rhs[:, c, :],
                                       start=c == 0, stop=c == kc - 1)
    last.then_inc(st.filling(name), 1)


def token_major(st, name, lhs, w, kc=DC, base=0):
    o = flat(st.claim(name)[:])
    for t in range(NT):
        for c in range(kc):
            last = st.nc.tensor.matmul(o[:, t * D:t * D + D], lhs[:, base + c, t * P:t * P + P], w[:, base + c, :],
                                       start=c == 0, stop=c == kc - 1)
    last.then_inc(st.filling(name), 1)


class Norm:

    def __init__(self, st, s):
        self.st, self.s = st, s
        self.stats = st.sb(f"stats{s}", [NT, 6])
        self.mv = st.sb(f"mv{s}", [NT, 2])
        self.rstd = st.sb(f"rstd{s}", [NT])
        self.var = st.sb(f"var{s}", [NT])
        self.asked = self.given = 0

    def vector(self, dve, nth, src, dst, ready, rms=False):
        nc, st, s = self.st.nc, self.st, self.s
        self.asked += 1
        for t in range(NT):
            last = nc.vector.bn_stats(self.stats[:, t, :], src[:, t, :])
        last.then_inc(st.sem("dve_step"), 1)
        dve.wait_ge(st.sem("dve_step"), nth())
        for t in range(NT):
            last = nc.vector.bn_aggr(self.mv[:, t, :], self.stats[:, t, :])
        last.then_inc(st.sem("dve_step"), 1)
        dve.wait_ge(st.sem("dve_step"), nth())
        var = self.mv[:, :, 1]
        if rms:
            nc.vector.tensor_tensor(self.var[:], self.mv[:, :, 0], self.mv[:, :, 0], ALU.mult).then_inc(
                st.sem("dve_step"), 1)
            dve.wait_ge(st.sem("dve_step"), nth())
            nc.vector.tensor_tensor(self.var[:], self.var[:], var, ALU.add).then_inc(st.sem(f"var{s}"), 1)
        else:
            nc.vector.tensor_copy(self.var[:], var).then_inc(st.sem(f"var{s}"), 1)
        dve.wait_ge(st.sem(f"rstd{s}"), self.asked)
        for t in range(NT):
            if rms:
                last = nc.vector.tensor_scalar(dst[:, t, :], src[:, t, :], self.rstd[:, t:t + 1], None, ALU.mult)
            else:
                last = nc.vector.tensor_scalar(dst[:, t, :], src[:, t, :], self.mv[:, t, 0:1],
                                               self.rstd[:, t:t + 1], ALU.subtract, ALU.mult)
        last.then_inc(st.sem(ready), 1)

    def gpsimd(self, pool, nth, neg_half, eps):
        nc, st, s = self.st.nc, self.st, self.s
        self.given += 1
        pool.wait_ge(st.sem(f"var{s}"), self.given)
        nc.gpsimd.tensor_scalar(self.rstd[:], self.var[:], eps, None, ALU.add).then_inc(st.sem("pool_step"), 1)
        pool.wait_ge(st.sem("pool_step"), nth())
        nc.gpsimd.tensor_tensor(self.rstd[:], self.rstd[:], neg_half[:, 0:NT], ALU.pow).then_inc(
            st.sem(f"rstd{s}"), 1)


def tokens(a, b):
    return a[bass.ds(b, 1), :, :].rearrange("a (t p) d -> p (a t) d", p=P)


def features(a, b):
    return a[bass.ds(b, 1), :, :].rearrange("a (c p) n -> p (a c) n", p=P)


def tiles_of(w):
    return w.rearrange("(c p) n -> p c n", p=P)


def copy_xT(st, act, name, xT, w=None, bias=None):
    act.wait_ge(*st.full(name))
    o = st.region(name)
    for c in range(DC):
        if w is None:
            last = st.nc.scalar.activation(xT[:, c, :], o[:, c, :], ACT.Copy)
        else:
            last = st.nc.scalar.activation(xT[:, c, :], o[:, c, :], ACT.Identity, scale=w[:, c:c + 1],
                                           bias=0.0 if bias is None else bias[:, c:c + 1])
    last.then_inc(st.emptying(name), 1)


def gla_layer(nc, A, K, psum, x_in, x_out, weights, SLOTS):
    with ExitStack() as ctx:
        st = Stage(nc, ctx, "gla", psum, K["sems"])
        ident, tri = K["ident"], K["tri"]
        wq, wk, wv, wg, wo, wgk1, wgk2, w1, w2 = (weights[n] for n in
                                                  ("Wq", "Wk", "Wv", "Wg", "Wo", "Wgk1", "Wgk2", "W1", "W2"))
        SL = range(SLOTS)
        bufs = []
        for s in SL:
            Z = {}
            for name, n in (("x", 4), ("xn", 4), ("x1", 4), ("res", 4)):
                Z[name] = st.sb(f"{name}{s}", [NT, D])
            xT = Z["xT"] = st.sb(f"xT{s}", [DC, T])
            ar = st.sb(f"work{s}", [42 * 256])

            def at(kb, n, ar=ar):
                return ar[:, kb * 256:kb * 256 + n]

            Z["q"], Z["sg"], Z["v"] = f3(at(0, 1024), DC), f3(at(4, 1024), DC), f3(at(8, 1024), NT)
            Z["k"] = f3(at(12, 1024), DC)
            Z["L"], Z["z"], Z["E1"], Z["Eq"] = at(16, 1024), at(20, 1024), at(24, 1024), at(28, 1024)
            Z["kp"], o = [], 32 * 256
            for i in range(NSUB):
                n = SUB * (i + 1)
                Z["kp"].append(ar[:, o:o + 8 * n].rearrange("p (a n) -> p a n", a=8))
                o += 8 * n
            Z["lowT"] = Z["kp"][3][:, 0:4, :].rearrange("p a n -> p (a n)")
            Z["kdec"], Z["kdT"] = at(12, 1024), f3(at(20, 1024), DC)
            Z["osb"], Z["osq"], Z["og"] = at(0, 1024), at(12, 1024), f3(at(16, 1024), DC)
            Z["hid"], Z["hid2"] = f3(at(0, 3072), HF), f3(at(12, 3072), HF)
            Z["eT"], Z["eF"], Z["orms"] = st.sb(f"eT{s}", [8]), st.sb(f"eF{s}", [8]), st.sb(f"orms{s}", [16])
            Z["Hs"] = st.sb(f"Hs{s}", [NT - 1, DC, P])
            Z["ats"] = st.sb(f"ats{s}", [2, 2, DC, P])
            Z["norm"] = Norm(st, s)
            bufs.append(Z)

        with nc.Block() as block:
            @block.vector
            def _(dve):
                nth = counter()
                for s in SL:
                    nc.vector.memset(bufs[s]["Hs"][:], 0.0).then_inc(st.sem("zeroed"), 1)
                    dve.wait_ge(st.sem("zeroed"), nth())
                    nc.vector.memset(bufs[s]["ats"][:], 0.0).then_inc(st.sem("zeroed"), 1)
                    dve.wait_ge(st.sem("zeroed"), nth())

            @block.sync
            def _(sp):
                weights.arrive(sp)
        st.zero_sems()

        with nc.Fori(0, B // SLOTS) as turn:
            with nc.Block() as block:
                @block.tensor
                def _(pe):
                    for s in SL:
                        pe.wait_ge(st.sem(f"xn{s}"), 1)
                        transposes(st, pe, f"ln1T{s}", bufs[s]["xn"], ident[:])
                    for s in SL:
                        xT = bufs[s]["xT"]
                        pe.wait_ge(*st.emptied(f"ln1T{s}"))
                        feature_major(st, f"low{s}", wgk1, 0, xT, tiles=1, m=LOW)
                        feature_major(st, f"q{s}", wq, 0, xT)
                        feature_major(st, f"k{s}", wk, 0, xT)
                        pe.wait_ge(*st.emptied(f"low{s}"))
                        o = st.claim(f"z{s}")
                        for c in range(DC):
                            last = nc.tensor.matmul(o[:, c, :], wgk2[0:LOW, 0, c * P:c * P + P],
                                                    bufs[s]["lowT"][0:LOW, :], start=True, stop=True)
                        last.then_inc(st.filling(f"z{s}"), 1)
                        feature_major(st, f"g{s}", wg, 0, xT)
                        token_major(st, f"v{s}", xT, wv)
                    for s in SL:
                        Z = bufs[s]
                        pe.wait_ge(st.sem(f"kdec{s}"), 1)
                        o = st.claim(f"kdT{s}")
                        for c in range(DC):
                            for t in range(NT):
                                last = nc.tensor.transpose(o[:, c, t * P:t * P + P], f3(Z["kdec"], 8)[:, c * NT + t, :],
                                                           ident[:])
                        last.then_inc(st.filling(f"kdT{s}"), 1)
                    for s in SL:
                        Z = bufs[s]
                        kp, Eq, E1, ats, v, Hs = Z["kp"], f3(Z["Eq"], DC), f3(Z["E1"], DC), Z["ats"], Z["v"], Z["Hs"]
                        pe.wait_ge(*st.emptied(f"v{s}"))
                        pe.wait_ge(*st.emptied(f"kdT{s}"))
                        for i in range(NT - 1):
                            o = st.claim(f"dh{s}_{i}")
                            for c in range(DC):
                                last = nc.tensor.matmul(o[:, 0, c * P:c * P + P], Z["kdT"][:, c, i * P:i * P + P],
                                                        v[:, i, c * P:c * P + P], start=True, stop=True)
                            last.then_inc(st.filling(f"dh{s}_{i}"), 1)
                        pe.wait_ge(st.sem(f"qdec{s}"), 1)

                        def scores(i):
                            o = st.claim(f"at{s}_{i}")
                            for j in range(NSUB):
                                for h in range(GH):
                                    r, c, n, to = 64 * (h % 2), h // 2, SUB * (j + 1), i * P + j * SUB
                                    last = nc.tensor.matmul(o[0:n, h % 2, c * P + j * SUB:c * P + j * SUB + SUB],
                                                            kp[j][r:r + 64, c * NT + i, :], Eq[r:r + 64, c, to:to + SUB],
                                                            start=True, stop=True)
                            last.then_inc(st.filling(f"at{s}_{i}"), 1)

                        oo = flat(st.claim(f"o{s}", long=True)[:])
                        scores(0)
                        for i in range(NT):
                            if i + 1 < NT:
                                scores(i + 1)
                            pe.wait_ge(*st.emptied(f"at{s}_{i}"))
                            if i:
                                pe.wait_ge(*st.emptied(f"dh{s}_{i - 1}"))
                            for c in range(DC):
                                if i:
                                    nc.tensor.matmul(oo[:, i * D + c * P:i * D + c * P + P], E1[:, c, i * P:i * P + P],
                                                     Hs[:, i - 1, c, :], start=True, stop=False)
                                for h in (2 * c, 2 * c + 1):
                                    last = nc.tensor.matmul(oo[:, i * D + 64 * h:i * D + 64 * h + 64],
                                                            ats[:, i % 2, h % 2, c, :], v[:, i, 64 * h:64 * h + 64],
                                                            start=i == 0, stop=i == 0 or h == 2 * c + 1)
                            if i < NT - 1:
                                last.then_inc(st.sem(f"o_part{s}"), 1)
                        last.then_inc(st.filling(f"o{s}"), 1)
                    for s in SL:
                        pe.wait_ge(st.sem(f"on{s}"), 1)
                        transposes(st, pe, f"onT{s}", bufs[s]["xn"], ident[:])
                    for s in SL:
                        pe.wait_ge(*st.emptied(f"onT{s}"))
                        token_major(st, f"attn{s}", bufs[s]["og"], wo)
                    for s in SL:
                        pe.wait_ge(st.sem(f"xn{s}"), 2)
                        transposes(st, pe, f"ln2T{s}", bufs[s]["xn"], ident[:])
                    for s in SL:
                        pe.wait_ge(*st.emptied(f"ln2T{s}"))
                        for i in range(HF // 2):
                            feature_major(st, f"mlp{s}_{i}", w1, 2 * i * P, bufs[s]["xT"])
                    for s in SL:
                        pe.wait_ge(st.sem(f"hid{s}"), HF // 2)
                        token_major(st, f"out{s}", bufs[s]["hid2"], w2, kc=HF)

                @block.sync
                def _(sp):
                    for s in SL:
                        sp.dma_start(bufs[s]["x"][:], tokens(x_in, turn * SLOTS + s)).then_inc(st.sem(f"x_in{s}"), 16)
                    for s in SL:
                        sp.wait_ge(st.sem(f"x_out{s}"), 1)
                        sp.dma_start(tokens(x_out, turn * SLOTS + s), bufs[s]["x"][:]).then_inc(st.sem("stored"), 16)
                    sp.wait_ge(st.sem("stored"), 16 * SLOTS)

                @block.scalar
                def _(act):
                    nth = counter()
                    A_ = nc.scalar.activation
                    ln1w, ln1b, ln2w, ln2b, b1, bgk2 = (K[n] for n in ("ln1_w", "ln1_b", "ln2_w", "ln2_b", "b1", "bgk2"))
                    for s in SL:
                        copy_xT(st, act, f"ln1T{s}", bufs[s]["xT"], ln1w, ln1b)
                    for s in SL:
                        Z = bufs[s]
                        act.wait_ge(*st.full(f"low{s}"))
                        o = st.region(f"low{s}")
                        A_(Z["lowT"][0:LOW, :], o[0:LOW, 0, :], ACT.Copy).then_inc(st.emptying(f"low{s}"), 1)
                        act.wait_ge(*st.full(f"q{s}"))
                        o = st.region(f"q{s}")
                        A_(Z["q"], o[:], ACT.Copy, scale=64 ** -0.5).then_inc(st.emptying(f"q{s}"), 1)
                        act.wait_ge(*st.full(f"z{s}"))
                        o = st.region(f"z{s}")
                        z = f3(Z["z"], DC)
                        for c in range(DC):
                            last = A_(z[:, c, :], o[:, c, :], ACT.Abs, bias=bgk2[:, c:c + 1])
                        last.then_inc(st.sem(f"z_abs{s}"), 1)
                        act.wait_ge(st.sem(f"z_abs{s}"), 1)
                        act.wait_ge(*st.full(f"g{s}"))
                        o = st.region(f"g{s}")
                        A_(Z["sg"], o[:], ACT.Silu).then_inc(st.emptying(f"g{s}"), 1)
                        A_(Z["z"], Z["z"], ACT.Exp, scale=-1.0).then_inc(st.sem("act_step"), 1)
                        act.wait_ge(st.sem("act_step"), nth())
                        A_(Z["z"], Z["z"], ACT.Ln, bias=1.0).then_inc(st.sem(f"softplus{s}"), 1)
                    for s in SL:
                        Z = bufs[s]
                        act.wait_ge(st.sem(f"logs{s}"), 1)
                        for kp in reversed(Z["kp"]):
                            A_(kp, kp, ACT.Exp, scale=1.0 / 16)
                        A_(Z["eF"][:], Z["eF"][:], ACT.Exp, scale=1.0 / 16)
                        A_(Z["Eq"], Z["Eq"], ACT.Exp, scale=1.0 / 16)
                        A_(Z["E1"], Z["L"], ACT.Exp, scale=1.0 / 16).then_inc(st.sem(f"exps{s}"), 1)
                    for s in SL:
                        Z = bufs[s]
                        act.wait_ge(*st.full(f"o{s}"))
                        o = flat(st.region(f"o{s}")[:])
                        A_(Z["osq"], o, ACT.Square).then_inc(st.sem(f"o_sq{s}"), 1)
                        A_(Z["osb"], o, ACT.Copy).then_inc(st.emptying(f"o{s}"), 1)
                    for s in SL:
                        copy_xT(st, act, f"ln2T{s}", bufs[s]["xT"], ln2w, ln2b)
                    for s in SL:
                        hid = bufs[s]["hid"]
                        for i in range(HF // 2):
                            act.wait_ge(*st.full(f"mlp{s}_{i}"))
                            o = st.region(f"mlp{s}_{i}")
                            A_(hid[:, 2 * i, :], o[:, 0, :], ACT.Identity, bias=b1[:, 2 * i:2 * i + 1])
                            A_(hid[:, 2 * i + 1, :], o[:, 1, :], ACT.Identity,
                               bias=b1[:, 2 * i + 1:2 * i + 2]).then_inc(st.emptying(f"mlp{s}_{i}"), 1)
                    for s in SL:
                        hid2 = bufs[s]["hid2"]
                        for i in range(HF // 2):
                            act.wait_ge(st.sem(f"leaky{s}"), i + 1)
                            A_(hid2[:, 2 * i:2 * i + 2, :], hid2[:, 2 * i:2 * i + 2, :], ACT.Square).then_inc(
                                st.sem(f"hid{s}"), 1)

                @block.vector
                def _(dve):
                    nth = counter()
                    V = nc.vector
                    bgk2, rmsw, resetting = K["bgk2"], K["rms_w"], K["chunk_mask"]
                    for s in SL:
                        Z = bufs[s]
                        dve.wait_ge(st.sem(f"x_in{s}"), 16)
                        Z["norm"].vector(dve, nth, Z["x"], Z["xn"], f"xn{s}")
                    for s in SL:
                        Z = bufs[s]
                        dve.wait_ge(*st.full(f"k{s}"))
                        o = st.region(f"k{s}")
                        V.tensor_copy(Z["k"], o[:]).then_inc(st.emptying(f"k{s}"), 1)
                        dve.wait_ge(*st.full(f"z{s}"))
                        o = st.region(f"z{s}")
                        dve.wait_ge(st.sem(f"z_abs{s}"), 1)
                        E1, L = f3(Z["E1"], DC), f3(Z["L"], DC)
                        for c in range(DC):
                            last = V.tensor_scalar(E1[:, c, :], o[:, c, :], bgk2[:, c:c + 1], 0.0, ALU.add, ALU.min)
                        last.then_inc(st.emptying(f"z{s}"), 1)
                        dve.wait_ge(*st.full(f"v{s}"))
                        o = st.region(f"v{s}")
                        V.tensor_copy(Z["v"], flat(o[:]).rearrange("p (t n) -> p t n", t=NT)).then_inc(
                            st.emptying(f"v{s}"), 1)
                        dve.wait_ge(st.sem(f"softplus{s}"), 1)
                        dve.wait_ge(*st.emptied(f"z{s}"))
                        V.tensor_tensor(Z["z"], Z["E1"], Z["z"], ALU.subtract).then_inc(st.sem("dve_step"), 1)
                        dve.wait_ge(st.sem("dve_step"), nth())
                        for c in range(DC):
                            last = V.tensor_tensor_scan(L[:, c, :], resetting[:], f3(Z["z"], DC)[:, c, :], 0.0,
                                                        ALU.mult, ALU.add)
                        last.then_inc(st.sem("dve_step"), 1)
                        dve.wait_ge(st.sem("dve_step"), nth())
                        Lt, Lb = f3(Z["L"], 8), f3(Z["L"], 8 * NSUB)
                        mid = SUB // 2 - 1
                        V.tensor_tensor(f3(Z["Eq"], 8 * NSUB), Lb, Lb[:, :, mid:mid + 1].to_broadcast([P, 8 * NSUB, SUB]),
                                        ALU.subtract)
                        V.tensor_tensor(Z["eF"][:], Lt[:, :, P - 1], Lt[:, :, P - SUB + mid], ALU.subtract)
                        for j in range(NSUB):
                            n = SUB * (j + 1)
                            to = j * SUB + mid
                            last = V.tensor_tensor(Z["kp"][j], Lt[:, :, to:to + 1].to_broadcast([P, 8, n]), Lt[:, :, 0:n],
                                                   ALU.subtract)
                        last.then_inc(st.sem(f"logs{s}"), 1)
                    for s in SL:
                        Z = bufs[s]
                        dve.wait_ge(st.sem(f"exps{s}"), 1)
                        kt = f3(flat(Z["k"]), 8)
                        V.tensor_tensor(Z["kp"][NSUB - 1], kt, Z["kp"][NSUB - 1], ALU.mult).then_inc(
                            st.sem("dve_step"), 1)
                        dve.wait_ge(st.sem("dve_step"), nth())
                        for j in range(NSUB - 1):
                            V.tensor_tensor(Z["kp"][j], kt[:, :, 0:SUB * (j + 1)], Z["kp"][j], ALU.mult)
                        V.tensor_copy(Z["eT"][:], f3(Z["E1"], 8)[:, :, P - 1]).then_inc(st.sem("dve_step"), 1)
                        dve.wait_ge(st.sem("dve_step"), nth())
                        V.tensor_tensor(f3(Z["kdec"], 8), Z["kp"][NSUB - 1], over(Z["eF"][:], P), ALU.mult).then_inc(
                            st.sem(f"kdec{s}"), 1)
                        dve.wait_ge(st.sem(f"kdec{s}"), 1)
                        dve.wait_ge(*st.emptied(f"q{s}"))
                        V.tensor_tensor(Z["Eq"], Z["Eq"], flat(Z["q"]), ALU.mult)
                        V.tensor_tensor(Z["E1"], Z["E1"], flat(Z["q"]), ALU.mult).then_inc(st.sem(f"qdec{s}"), 1)
                    for s in SL:
                        Z = bufs[s]
                        dve.wait_ge(*st.full(f"kdT{s}"))
                        o = st.region(f"kdT{s}")
                        V.tensor_copy(Z["kdT"], o[:]).then_inc(st.emptying(f"kdT{s}"), 1)
                    for s in SL:
                        Z = bufs[s]
                        Hs, eT = Z["Hs"], Z["eT"]

                        def mask_scores(i):
                            dve.wait_ge(*st.full(f"at{s}_{i}"))
                            o = st.region(f"at{s}_{i}")
                            if i >= 2:
                                dve.wait_ge(st.sem(f"o_part{s}"), i - 1)
                            causal = tri[:].bitcast(U32).unsqueeze(1).unsqueeze(1).to_broadcast([P, 2, DC, P])
                            V.copy_predicated(Z["ats"][:, i % 2, :, :, :], causal,
                                              o[:, :, 0:D].rearrange("p r (c n) -> p r c n", c=DC)).then_inc(
                                                  st.emptying(f"at{s}_{i}"), 1)

                        for i in range(NT - 1):
                            dve.wait_ge(*st.full(f"dh{s}_{i}"))
                            o = st.region(f"dh{s}_{i}")
                            for c in range(DC):
                                for r in (0, 64):
                                    src, dst = o[r:r + 64, 0, c * P + r:c * P + r + 64], Hs[r:r + 64, i, c, r:r + 64]
                                    if i:
                                        last = V.scalar_tensor_tensor(dst, Hs[r:r + 64, i - 1, c, r:r + 64],
                                                                      eT[r:r + 64, c * NT + i:c * NT + i + 1], src,
                                                                      ALU.mult, ALU.add)
                                    else:
                                        last = V.tensor_copy(dst, src)
                            last.then_inc(st.emptying(f"dh{s}_{i}"), 1)
                            dve.wait_ge(*st.emptied(f"dh{s}_{i}"))
                        for i in range(NT):
                            mask_scores(i)
                    for s in SL:
                        Z = bufs[s]
                        dve.wait_ge(st.sem(f"o_sq{s}"), 1)
                        V.tensor_reduce(Z["orms"][:], f3(Z["osq"], 16), AX, ALU.add).then_inc(st.sem(f"o_ms{s}"), 1)
                        dve.wait_ge(st.sem(f"o_rms{s}"), 1)
                        dve.wait_ge(*st.emptied(f"o{s}"))
                        V.tensor_tensor(f3(flat(Z["xn"][:]), 16), f3(Z["osb"], 16), over(Z["orms"][:], 64),
                                        ALU.mult).then_inc(st.sem(f"on{s}"), 1)
                    for s in SL:
                        Z = bufs[s]
                        dve.wait_ge(*st.full(f"onT{s}"))
                        o = st.region(f"onT{s}")
                        dve.wait_ge(*st.emptied(f"g{s}"))
                        V.scalar_tensor_tensor(Z["og"], o[:], rmsw[:, 0:1], Z["sg"], ALU.mult, ALU.mult).then_inc(
                            st.emptying(f"onT{s}"), 1)
                    for s in SL:
                        Z = bufs[s]
                        dve.wait_ge(*st.full(f"attn{s}"))
                        o = st.region(f"attn{s}")
                        V.tensor_tensor(flat(Z["x1"][:]), flat(Z["x"][:]), flat(o[:]), ALU.add).then_inc(
                            st.emptying(f"attn{s}"), 1)
                        dve.wait_ge(*st.emptied(f"attn{s}"))
                        Z["norm"].vector(dve, nth, Z["x1"], Z["xn"], f"xn{s}")
                    for s in SL:
                        Z = bufs[s]
                        for i in range(HF // 2):
                            dve.wait_ge(*st.emptied(f"mlp{s}_{i}"))
                            h = Z["hid"][:, 2 * i:2 * i + 2, :]
                            V.scalar_tensor_tensor(Z["hid2"][:, 2 * i:2 * i + 2, :], h, 0.01, h,
                                                   ALU.mult, ALU.max).then_inc(st.sem(f"leaky{s}"), 1)
                    for s in SL:
                        Z = bufs[s]
                        dve.wait_ge(*st.full(f"out{s}"))
                        o = st.region(f"out{s}")
                        dve.wait_ge(st.sem(f"res{s}"), 1)
                        V.tensor_tensor(flat(Z["res"][:]), flat(Z["res"][:]), flat(o[:]), ALU.add).then_inc(
                            st.emptying(f"out{s}"), 1)
                        dve.wait_ge(*st.emptied(f"out{s}"))
                        Z["norm"].vector(dve, nth, Z["res"], Z["x"], f"x_out{s}")

                @block.gpsimd
                def _(pool):
                    nth = counter()
                    G = nc.gpsimd
                    for s in SL:
                        bufs[s]["norm"].gpsimd(pool, nth, K["neg_half"], 1e-5)
                    for s in SL:
                        Z = bufs[s]
                        pool.wait_ge(st.sem(f"x_in{s}"), 16)
                        G.tensor_tensor(Z["res"][:], Z["x"][:], times(K["b2"], NT), ALU.add).then_inc(
                            st.sem("pool_step"), 1)
                        pool.wait_ge(st.sem("pool_step"), nth())
                    for s in SL:
                        Z = bufs[s]
                        pool.wait_ge(st.sem(f"o_ms{s}"), 1)
                        G.tensor_scalar(Z["orms"][:], Z["orms"][:], 1.0 / 64, 1e-5, ALU.mult, ALU.add).then_inc(
                            st.sem("pool_step"), 1)
                        pool.wait_ge(st.sem("pool_step"), nth())
                        G.tensor_tensor(Z["orms"][:], Z["orms"][:], K["neg_half"][:], ALU.pow).then_inc(
                            st.sem(f"o_rms{s}"), 1)
                    for s in SL:
                        Z = bufs[s]
                        Z["norm"].gpsimd(pool, nth, K["neg_half"], 1e-5)
                        G.tensor_tensor(Z["res"][:], Z["res"][:], Z["x1"][:], ALU.add).then_inc(st.sem(f"res{s}"), 1)
                    for s in SL:
                        bufs[s]["norm"].gpsimd(pool, nth, K["neg_half"], 1e-5)
            st.zero_sems()
def xattn_layer(nc, A, K, psum, x_in, x_out, weights, SLOTS):
    with ExitStack() as ctx:
        st = Stage(nc, ctx, "xattn", psum, K["sems"])
        ident = K["ident"]
        wq, wk, wv, wo = (weights[n] for n in ("xwq", "xwk", "xwv", "xwo"))
        x, xT, ctxT = st.sb("x", [NT, D]), st.sb("xT", [DC, T]), st.sb("ctxT", [DC, T])
        qf, kf = st.sb("qf", [DC, T]), st.sb("kf", [DC, T])
        qhi, qlo, khi, klo = (st.sb(n, [DC, T], F32R) for n in ("qhi", "qlo", "khi", "klo"))
        q1, q2 = st.sb("q1", [2, 2, T], F32R), st.sb("q2", [2, 2, T], F32R)
        ks = st.sb("ks", [2, 4, T], F32R)
        va = st.sb("va", [NT, XH, 32])
        probs = st.sb("probs", [4, 2, T])
        neg_max = st.sb("neg_max", [2, NT, 2])
        placed = st.sb("placed", [2, NT, P], F32R)
        o_T, attn, attnT = st.sb("o_T", [T]), st.sb("attn", [NT, D]), st.sb("attnT", [DC, T])
        recip = st.sb("recip", [NT, 4])
        sel = {n: st.sb("sel_" + n, [4, P], F32R) for n in ("qhi", "qlo", "khi", "klo")}
        identr = st.sb("identr", [P], F32R)
        half_mask, half_bias, q_bias = st.sb("half_mask", [2]), st.sb("half_bias", [2]), st.sb("q_bias", [DC])
        norm = Norm(st, 0)

        with nc.Block() as block:
            @block.vector
            def _(dve):
                nth = counter()
                V = nc.vector
                zeros = K["chunk_mask"][:].rearrange("p (a n) -> p a n", a=4)
                for t in sel.values():
                    last = V.tensor_scalar(t[:], zeros, 0.0, None, ALU.mult)
                last.then_inc(st.sem("dve_step"), 1)
                dve.wait_ge(st.sem("dve_step"), nth())
                for a in range(2):
                    V.tensor_scalar(placed[:, a, :, :], zeros, 0.0, None, ALU.mult)
                V.memset(va[:, :, :, 17:32], 0.0)
                V.memset(va[:, :, :, 16:17], 1.0)
                V.tensor_copy(identr[:], ident[:])
                V.tensor_scalar(q_bias[:], K["xwq_b"], 0.25, None, ALU.mult)
                source = ident[:].rearrange("p (a r m) -> p a r m", a=4, r=2)
                for n, blocks in (("qhi", (0, 1)), ("qlo", (2,)), ("khi", (0, 2)), ("klo", (1,))):
                    for k in blocks:
                        for r in range(2):
                            V.tensor_copy(sel[n][:, :, 64 * r + 16 * k:64 * r + 16 * k + 16], source[:, :, r, :])

            @block.gpsimd
            def _(pool):
                nth = counter()
                G = nc.gpsimd
                G.memset(half_bias[:], 0.0).then_inc(st.sem("pool_step"), 1)
                pool.wait_ge(st.sem("pool_step"), nth())
                G.memset(half_mask[:], 0.0).then_inc(st.sem("pool_step"), 1)
                pool.wait_ge(st.sem("pool_step"), nth())
                for r in range(2):
                    G.memset(half_mask[64 * r:64 * r + 64, r:r + 1], 1.0).then_inc(st.sem("pool_step"), 1)
                    pool.wait_ge(st.sem("pool_step"), nth())
                    for m in (48, 49):
                        G.affine_select(out=half_bias[:, r:r + 1], in_=half_bias[:, r:r + 1],
                                        compare_op=ALU.not_equal, fill=1.0, base=-(64 * r + m),
                                        pattern=[[0, 1]], channel_multiplier=1).then_inc(st.sem("pool_step"), 1)
                        pool.wait_ge(st.sem("pool_step"), nth())

            @block.sync
            def _(sp):
                weights.arrive(sp)
        st.zero_sems()

        steps = [(a, i) for a in range(2) for i in range(NT)]
        LAG = 2

        with nc.Fori(0, B // SLOTS) as turn:
            with nc.Block() as block:
                @block.tensor
                def _(pe):
                    mm, tr = nc.tensor.matmul, nc.tensor.transpose

                    def stack(name, hi, lo, qd, maxima=False):
                        o = st.claim(name)
                        for a in range(2):
                            c, pattern = divmod(2 * qd + a, 4)
                            h, l = (qhi, qlo) if hi == "qhi" else (khi, klo)
                            mm(o[:, a, :], sel[hi][:, pattern, :], h[:, c, :], start=True, stop=False)
                            last = mm(o[:, a, :], sel[lo][:, pattern, :], l[:, c, :], start=False, stop=not maxima)
                            if maxima:
                                for t in range(NT):
                                    last = mm(o[:, a, t * P:t * P + P], placed[:, a, t, :], identr[:], start=False,
                                              stop=t == NT - 1)
                        last.then_inc(st.filling(name), 1)

                    def prepare(qd):
                        stack(f"q1_{qd}", "qhi", "qlo", qd)
                        stack(f"ks_{qd}", "khi", "klo", qd)
                        pe.wait_ge(*st.emptied(f"q1_{qd}"))
                        pe.wait_ge(*st.emptied(f"ks_{qd}"))

                    def by_queries(qd, a, t):
                        o = st.claim(f"s{qd}_{a}_{t}")
                        for r in range(2):
                            last = mm(o[:, r, :], q1[:, qd % 2, a, t * P:t * P + P], ks[:, qd % 2, 2 * a + r, :],
                                      start=True, stop=True)
                        last.then_inc(st.filling(f"s{qd}_{a}_{t}"), 1)

                    def by_keys(qd, a, j):
                        o = st.claim(f"sT{qd}_{a}_{j}")
                        for r in range(2):
                            last = mm(o[:, r, :], ks[:, qd % 2, 2 * a + r, j * P:j * P + P], q2[:, qd % 2, a, :],
                                      start=True, stop=True)
                        last.then_inc(st.filling(f"sT{qd}_{a}_{j}"), 1)

                    def values(o, qd, a, j):
                        pe.wait_ge(*st.emptied(f"sT{qd}_{a}_{j}"))
                        for r in range(2):
                            g = 2 * a + r
                            last = mm(o[32 * g:32 * g + 32, 0, :], va[:, j, 4 * qd + g, :],
                                      probs[:, (NT * a + j) % 4, r, :], start=j == 0, stop=j == NT - 1)
                        return last

                    def with_maxima(qd):
                        pe.wait_ge(st.sem("placed"), qd + 1)
                        stack(f"q2_{qd}", "qhi", "qlo", qd, maxima=True)

                    def out_tokens(qd):
                        pe.wait_ge(*st.emptied(f"pv{qd}"))
                        o = st.claim(f"o{qd}")
                        for t in range(NT):
                            last = tr(o[:, 0, t * P:t * P + P], o_T[:, t * P:t * P + P], ident[:])
                        last.then_inc(st.filling(f"o{qd}"), 1)

                    pe.wait_ge(st.sem("x_in"), 16)
                    transposes(st, pe, "xT", x, ident[:])
                    pe.wait_ge(st.sem("ctx_in"), 16)
                    feature_major(st, "k", wk, 0, ctxT)
                    pe.wait_ge(*st.emptied("xT"))
                    feature_major(st, "q", wq, 0, xT)
                    token_major(st, "v", ctxT, wv)
                    pe.wait_ge(st.sem("split"), 2)
                    prepare(0)
                    for a, t in steps:
                        by_queries(0, a, t)
                    with_maxima(0)
                    for qd in range(XQ):
                        ahead = qd + 1 < XQ
                        if ahead:
                            prepare(qd + 1)
                        pe.wait_ge(*st.emptied(f"q2_{qd}"))
                        if qd == 0:
                            pe.wait_ge(*st.emptied("v"))
                        long = None
                        for i in range(len(steps) + LAG):
                            if i < len(steps):
                                by_keys(qd, *steps[i])
                                if ahead:
                                    by_queries(qd + 1, *steps[i])
                                if qd and i == 2:
                                    out_tokens(qd - 1)
                            if i >= LAG:
                                if long is None:
                                    long = st.claim(f"pv{qd}", long=True)
                                last = values(long, qd, *steps[i - LAG])
                                if i - LAG < len(steps) - 1:
                                    last.then_inc(st.sem("probs_used"), 1)
                        last.then_inc(st.filling(f"pv{qd}"), 1)
                        if ahead:
                            with_maxima(qd + 1)
                    out_tokens(XQ - 1)
                    pe.wait_ge(*st.emptied(f"o{XQ - 1}"))
                    transposes(st, pe, "attnT", attn, ident[:])
                    pe.wait_ge(*st.emptied("attnT"))
                    token_major(st, "out", attnT, wo)

                @block.sync
                def _(sp):
                    sp.dma_start(ctxT[:], features(A["ctxT"], turn)).then_inc(st.sem("ctx_in"), 16)
                    sp.dma_start(x[:], tokens(x_in, turn)).then_inc(st.sem("x_in"), 16)
                    sp.wait_ge(st.sem("x_out"), 1)
                    sp.dma_start(tokens(x_out, turn), x[:]).then_inc(st.sem("stored"), 16)
                    sp.wait_ge(st.sem("stored"), 16)

                @block.scalar
                def _(act):
                    A_ = nc.scalar.activation
                    copy_xT(st, act, "xT", xT)
                    for name, dst, hi, scale, bias in (("k", kf, khi, 1.0, K["xwk_b"]), ("q", qf, qhi, 0.25, q_bias)):
                        act.wait_ge(*st.full(name))
                        o = st.region(name)
                        for c in range(DC):
                            last = A_(dst[:, c, :], o[:, c, :], ACT.Identity, scale=scale, bias=bias[:, c:c + 1])
                        last.then_inc(st.emptying(name), 1)
                        act.wait_ge(*st.emptied(name))
                        A_(hi[:], dst[:], ACT.Copy).then_inc(st.sem("hi"), 1)

                    def keys(qd):
                        act.wait_ge(*st.full(f"ks_{qd}"))
                        o = st.region(f"ks_{qd}")
                        for h in range(4):
                            r = h % 2
                            last = A_(ks[:, qd % 2, h, :], o[:, h // 2, :], ACT.Identity, scale=half_mask[:, r:r + 1],
                                      bias=half_bias[:, r:r + 1])
                        last.then_inc(st.emptying(f"ks_{qd}"), 1)

                    def queries(qd):
                        act.wait_ge(*st.full(f"q2_{qd}"))
                        o = st.region(f"q2_{qd}")
                        A_(q2[:, qd % 2, :, :], o[:], ACT.Copy).then_inc(st.emptying(f"q2_{qd}"), 1)

                    keys(0)
                    queries(0)
                    for qd in range(XQ):
                        if qd + 1 < XQ:
                            keys(qd + 1)
                        for i, (a, j) in enumerate(steps):
                            act.wait_ge(*st.full(f"sT{qd}_{a}_{j}"))
                            o = st.region(f"sT{qd}_{a}_{j}")
                            if i >= 4:
                                act.wait_ge(st.sem("probs_used"), (len(steps) - 1) * qd + i - 3)
                            elif qd:
                                if i < 3:
                                    act.wait_ge(st.sem("probs_used"), (len(steps) - 1) * (qd - 1) + i + 5)
                                else:
                                    act.wait_ge(*st.full(f"pv{qd - 1}"))
                            A_(probs[:, i % 4, :, :], o[:], ACT.Exp).then_inc(st.emptying(f"sT{qd}_{a}_{j}"), 1)
                        if qd + 1 < XQ:
                            queries(qd + 1)
                    act.wait_ge(*st.full("attnT"))
                    o = st.region("attnT")
                    A_(attnT[:], o[:], ACT.Copy).then_inc(st.emptying("attnT"), 1)

                @block.vector
                def _(dve):
                    V = nc.vector
                    nth = counter()
                    for i, (f, hi, lo) in enumerate(((kf, khi, klo), (qf, qhi, qlo))):
                        dve.wait_ge(st.sem("hi"), i + 1)
                        V.tensor_tensor(lo[:], f[:], hi[:].bitcast(F32), ALU.subtract).then_inc(st.sem("split"), 1)
                    dve.wait_ge(*st.full("v"))
                    o = flat(st.region("v")[:])
                    for t in range(NT):
                        last = V.tensor_tensor(va[:, t, :, 0:16], f3(o[:, t * D:t * D + D], XH), f3(K["xwv_b"], XH),
                                               ALU.add)
                    last.then_inc(st.emptying("v"), 1)

                    def queries(qd):
                        dve.wait_ge(*st.full(f"q1_{qd}"))
                        o = st.region(f"q1_{qd}")
                        V.tensor_copy(q1[:, qd % 2, :, :], o[:]).then_inc(st.emptying(f"q1_{qd}"), 1)

                    def maxima(qd, a, t):
                        dve.wait_ge(*st.full(f"s{qd}_{a}_{t}"))
                        o = st.region(f"s{qd}_{a}_{t}")
                        V.tensor_reduce(neg_max[:, a, t, :], o[:], AX, ALU.max).then_inc(
                            st.emptying(f"s{qd}_{a}_{t}"), 1)

                    def place(qd):
                        dve.wait_ge(*st.emptied(f"s{qd}_1_{NT - 1}"))
                        dve.wait_ge(*st.emptied(f"s{qd}_1_{NT - 2}"))
                        dve.wait_ge(*st.emptied(f"s{qd}_1_{NT - 3}"))
                        cols = placed[:].rearrange("p a t (r m) -> p a t r m", r=2)
                        hi, lo = cols[:, :, :, :, 48], cols[:, :, :, :, 49]
                        for a in range(2):
                            last = V.tensor_scalar(hi[:, a], neg_max[:, a, :, :], -1.0, None, ALU.mult)
                        last.then_inc(st.sem("dve_step"), 1)
                        dve.wait_ge(st.sem("dve_step"), nth())
                        for a in range(2):
                            for r in range(2):
                                last = V.scalar_tensor_tensor(lo[:, a, :, r], neg_max[:, a, :, r], -1.0,
                                                              hi[:, a, :, r].bitcast(F32), ALU.mult, ALU.subtract)
                        last.then_inc(st.sem("placed"), 1)
                        dve.wait_ge(st.sem("placed"), qd + 1)

                    def normalised(qd):
                        dve.wait_ge(*st.full(f"o{qd}"))
                        o = f3(st.region(f"o{qd}")[:, 0, :], NT)
                        heads = o.rearrange("p t (h d) -> p t h d", h=4)
                        V.reciprocal(recip[:], heads[:, :, :, 16]).then_inc(st.sem("dve_step"), 1)
                        dve.wait_ge(st.sem("dve_step"), nth())
                        for t in range(NT):
                            last = V.tensor_tensor(f3(attn[:, t, 64 * qd:64 * qd + 64], 4), heads[:, t, :, 0:16],
                                                   over(recip[:, t, :], 16), ALU.mult)
                        last.then_inc(st.emptying(f"o{qd}"), 1)

                    queries(0)
                    for a, t in steps:
                        maxima(0, a, t)
                    place(0)
                    for qd in range(XQ):
                        ahead = qd + 1 < XQ
                        if ahead:
                            queries(qd + 1)
                        for i, (a, t) in enumerate(steps):
                            if ahead:
                                maxima(qd + 1, a, t)
                            if qd and i == 2:
                                normalised(qd - 1)
                        if ahead:
                            place(qd + 1)
                        dve.wait_ge(*st.full(f"pv{qd}"))
                        o = st.region(f"pv{qd}")
                        V.tensor_copy(o_T[:], o[:, 0, :]).then_inc(st.emptying(f"pv{qd}"), 1)
                    V.tensor_tensor(x[:], x[:], times(K["xwo_b"], NT), ALU.add).then_inc(st.sem("dve_step"), 1)
                    dve.wait_ge(st.sem("dve_step"), nth())
                    normalised(XQ - 1)
                    dve.wait_ge(*st.full("out"))
                    o = st.region("out")
                    V.tensor_tensor(flat(x[:]), flat(x[:]), flat(o[:]), ALU.add).then_inc(st.emptying("out"), 1)
                    dve.wait_ge(*st.emptied("out"))
                    norm.vector(dve, nth, x, x, "x_out")

                @block.gpsimd
                def _(pool):
                    norm.gpsimd(pool, counter(), K["neg_half"], 1e-5)
            st.zero_sems()
def route(nc, dve, nth, st, s, Z, rank8, part):
    V = nc.vector
    r, m = Z["rt"], Z["per_token"]

    def tile(i):
        return r[:, i, :, 0:NE]

    def spread(i, n=NE):
        return over(m[:, i, :], n)

    scores, masked, alive, size, work, work2 = tile(0), tile(1), tile(2), tile(3), tile(4), tile(5)
    PICK, KEEP, EXPO, RW, RUN, TAKEN, OUT, OPEN = 6, 10, 14, 18, 19, 20, 21, 22
    if part == 0:
        dve.wait_ge(*st.emptied(f"logits{s}"))
        V.memset(alive, 1.0)
        V.tensor_copy(masked, scores).then_inc(st.sem("dve_step"), 1)
        dve.wait_ge(st.sem("dve_step"), nth())
        V.scalar_tensor_tensor(size, scores, -1.0, scores, ALU.mult, ALU.max).then_inc(st.sem("dve_step"), 1)
        dve.wait_ge(st.sem("dve_step"), nth())
        for k in range(TOPK):
            V.tensor_reduce(m[:, k, :], masked, AX, ALU.max).then_inc(st.sem("dve_step"), 1)
            dve.wait_ge(st.sem("dve_step"), nth())
            V.tensor_tensor(work, masked, spread(k), ALU.is_equal).then_inc(st.sem("dve_step"), 1)
            dve.wait_ge(st.sem("dve_step"), nth())
            V.tensor_tensor(work, work, times(rank8[:], NT), ALU.mult).then_inc(st.sem("dve_step"), 1)
            dve.wait_ge(st.sem("dve_step"), nth())
            V.tensor_reduce(m[:, 4, :], work, AX, ALU.max).then_inc(st.sem("dve_step"), 1)
            dve.wait_ge(st.sem("dve_step"), nth())
            V.tensor_tensor(tile(PICK + k), work, spread(4), ALU.is_equal).then_inc(st.sem("dve_step"), 1)
            dve.wait_ge(st.sem("dve_step"), nth())
            V.tensor_tensor(work2, scores, spread(k), ALU.subtract).then_inc(st.sem("dve_step"), 1)
            dve.wait_ge(st.sem("dve_step"), nth())
            V.tensor_scalar(tile(EXPO + k), work2, 0.0, None, ALU.min).then_inc(st.sem("dve_step"), 1)
            dve.wait_ge(st.sem("dve_step"), nth())
            V.scalar_tensor_tensor(m[:, 4, :], m[:, k, :], -1.0, m[:, k, :], ALU.mult, ALU.max).then_inc(
                st.sem("dve_step"), 1)
            dve.wait_ge(st.sem("dve_step"), nth())
            V.tensor_tensor(work, size, spread(4), ALU.max).then_inc(st.sem("dve_step"), 1)
            dve.wait_ge(st.sem("dve_step"), nth())
            V.scalar_tensor_tensor(work, work, 2 * JITTER, work2, ALU.mult, ALU.add).then_inc(st.sem("dve_step"), 1)
            dve.wait_ge(st.sem("dve_step"), nth())
            V.scalar_tensor_tensor(tile(KEEP + k), work, 0.0, alive, ALU.is_ge, ALU.mult).then_inc(
                st.sem("dve_step"), 1)
            dve.wait_ge(st.sem("dve_step"), nth())
            V.scalar_tensor_tensor(masked, tile(PICK + k), -1e30, masked, ALU.mult, ALU.add).then_inc(
                st.sem("dve_step"), 1)
            dve.wait_ge(st.sem("dve_step"), nth())
            V.tensor_tensor(alive, alive, tile(PICK + k), ALU.subtract).then_inc(st.sem("dve_step"), 1)
            dve.wait_ge(st.sem("dve_step"), nth())
        V.tensor_copy(m[:, 5, :], m[:, 0, :]).then_inc(st.sem(f"expo{s}"), 1)
        dve.wait_ge(st.sem(f"exped{s}"), 1)
        E0 = tile(EXPO)
        V.tensor_reduce(m[:, 4, :], E0, AX, ALU.add).then_inc(st.sem("dve_step"), 1)
        dve.wait_ge(st.sem("dve_step"), nth())
        V.reciprocal(m[:, 4, :], m[:, 4, :]).then_inc(st.sem("dve_step"), 1)
        dve.wait_ge(st.sem("dve_step"), nth())
        for k in range(TOPK - 1):
            V.tensor_tensor(work, tile(PICK + k), E0, ALU.mult).then_inc(st.sem("dve_step"), 1)
            dve.wait_ge(st.sem("dve_step"), nth())
            V.tensor_reduce(m[:, 6 + k, :], work, AX, ALU.add).then_inc(st.sem("dve_step"), 1)
            dve.wait_ge(st.sem("dve_step"), nth())
        V.tensor_tensor(m[:, 6:9, :], m[:, 6:9, :], m[:, 4:5, :].to_broadcast([P, 3, NT]), ALU.mult).then_inc(
            st.sem("dve_step"), 1)
        dve.wait_ge(st.sem("dve_step"), nth())
        V.tensor_tensor(m[:, 7, :], m[:, 7, :], m[:, 6, :], ALU.add).then_inc(st.sem("dve_step"), 1)
        dve.wait_ge(st.sem("dve_step"), nth())
        V.tensor_tensor(m[:, 8, :], m[:, 8, :], m[:, 7, :], ALU.add).then_inc(st.sem("dve_step"), 1)
        dve.wait_ge(st.sem("dve_step"), nth())
        kept, expo = r[:, KEEP:KEEP + 4, :, 0:NE], r[:, EXPO:EXPO + 4, :, 0:NE]
        for k in range(TOPK):
            last = V.tensor_tensor(tile(KEEP + k), tile(KEEP + k), tile(EXPO + k), ALU.mult)
        last.then_inc(st.sem("dve_step"), 1)
        dve.wait_ge(st.sem("dve_step"), nth())
        for k in range(TOPK):
            last = V.tensor_reduce(m[:, 9 + k, :], tile(KEEP + k), AX, ALU.add)
        last.then_inc(st.sem("dve_step"), 1)
        dve.wait_ge(st.sem("dve_step"), nth())
        V.reciprocal(m[:, 9:13, :], m[:, 9:13, :]).then_inc(st.sem("dve_step"), 1)
        dve.wait_ge(st.sem("dve_step"), nth())
        V.scalar_tensor_tensor(m[:, 10:13, :], m[:, 6:9, :], TOP_P, m[:, 10:13, :], ALU.is_lt, ALU.mult).then_inc(
            st.sem("dve_step"), 1)
        dve.wait_ge(st.sem("dve_step"), nth())
        for k in range(TOPK):
            last = V.tensor_tensor(tile(KEEP + k), tile(PICK + k), spread(9 + k), ALU.mult)
        last.then_inc(st.sem("dve_step"), 1)
        dve.wait_ge(st.sem("dve_step"), nth())
        V.tensor_tensor(tile(RW), tile(KEEP), tile(KEEP + 1), ALU.add).then_inc(st.sem("dve_step"), 1)
        dve.wait_ge(st.sem("dve_step"), nth())
        V.tensor_tensor(tile(RW), tile(RW), tile(KEEP + 2), ALU.add).then_inc(st.sem("dve_step"), 1)
        dve.wait_ge(st.sem("dve_step"), nth())
        V.tensor_tensor(tile(RW), tile(RW), tile(KEEP + 3), ALU.add).then_inc(st.sem("dve_step"), 1)
        dve.wait_ge(st.sem("dve_step"), nth())
        V.tensor_reduce(m[:, 4, :], tile(RW), AX, ALU.add).then_inc(st.sem("dve_step"), 1)
        dve.wait_ge(st.sem("dve_step"), nth())
        V.reciprocal(m[:, 4, :], m[:, 4, :]).then_inc(st.sem("dve_step"), 1)
        dve.wait_ge(st.sem("dve_step"), nth())
        V.tensor_tensor(tile(RW), tile(RW), spread(4), ALU.mult).then_inc(st.sem("dve_step"), 1)
        dve.wait_ge(st.sem("dve_step"), nth())
        V.tensor_scalar(Z["mask"], tile(RW), 0.0, None, ALU.is_gt).then_inc(st.sem(f"mask{s}"), 1)
    else:
        carry = Z["carry"]
        dve.wait_ge(*st.full(f"count{s}"))
        o = st.region(f"count{s}")
        given, total = f3(o[:, 0, 0:32], NT), f3(o[:, 1, 0:32], NT)
        for t in range(NT):
            V.tensor_tensor(r[:, RUN, t, 0:NE], given[:, t, :], carry[:], ALU.add).then_inc(st.sem("dve_step"), 1)
            dve.wait_ge(st.sem("dve_step"), nth())
            last = V.tensor_tensor(carry[:], total[:, t, :], carry[:], ALU.add)
            if t < NT - 1:
                last.then_inc(st.sem("dve_step"), 1)
                dve.wait_ge(st.sem("dve_step"), nth())
        last.then_inc(st.emptying(f"count{s}"), 1)
        dve.wait_ge(st.sem(f"mask{s}"), 1)
        V.memset(r[:, TAKEN, :, :], 1.0)
        V.memset(r[:, OPEN, :, :], 0.0).then_inc(st.sem("dve_step"), 1)
        dve.wait_ge(st.sem("dve_step"), nth())
        V.scalar_tensor_tensor(tile(TAKEN), tile(RUN), CAP + 0.5, Z["mask"], ALU.is_le, ALU.mult).then_inc(
            st.sem("dve_step"), 1)
        dve.wait_ge(st.sem("dve_step"), nth())
        V.tensor_scalar(r[:, OPEN, :, :], r[:, TAKEN, :, :], 1e30, -1e30, ALU.mult, ALU.add).then_inc(
            st.sem("dve_step"), 1)
        dve.wait_ge(st.sem("dve_step"), nth())
        V.tensor_tensor(r[:, OUT, :, :], r[:, 0, :, :], r[:, TAKEN, :, :], ALU.mult).then_inc(st.sem("dve_step"), 1)
        dve.wait_ge(st.sem("dve_step"), nth())
        V.tensor_tensor(r[:, OUT, :, :], r[:, OUT, :, :], r[:, OPEN, :, :], ALU.add).then_inc(st.sem("dve_step"), 1)
        dve.wait_ge(st.sem("dve_step"), nth())
        V.tensor_reduce(m[:, 4, :], r[:, OUT, :, :], AX, ALU.max).then_inc(st.sem("dve_step"), 1)
        dve.wait_ge(st.sem("dve_step"), nth())
        V.tensor_tensor(r[:, OUT, :, :], r[:, OUT, :, :], spread(4, NE + 1), ALU.subtract).then_inc(
            st.sem("dve_step"), 1)
        dve.wait_ge(st.sem("dve_step"), nth())
        V.tensor_scalar(r[:, OUT, :, :], r[:, OUT, :, :], -200.0, None, ALU.max).then_inc(st.sem(f"expo{s}"), 1)
        dve.wait_ge(st.sem(f"exped{s}"), 2)
        V.tensor_reduce(m[:, 4, :], r[:, OUT, :, :], AX, ALU.add).then_inc(st.sem("dve_step"), 1)
        dve.wait_ge(st.sem("dve_step"), nth())
        V.tensor_reduce(m[:, 5, :], tile(OUT), AX, ALU.add).then_inc(st.sem("dve_step"), 1)
        dve.wait_ge(st.sem("dve_step"), nth())
        V.reciprocal(m[:, 4, :], m[:, 4, :]).then_inc(st.sem("dve_step"), 1)
        dve.wait_ge(st.sem("dve_step"), nth())
        V.tensor_tensor(m[:, 5, :], m[:, 5, :], m[:, 4, :], ALU.mult).then_inc(st.sem("dve_step"), 1)
        dve.wait_ge(st.sem("dve_step"), nth())
        V.tensor_tensor(r[:, OUT, :, NE:NE + 1], r[:, OUT, :, NE:NE + 1], m[:, 4, :].unsqueeze(2), ALU.mult).then_inc(
            st.sem("dve_step"), 1)
        dve.wait_ge(st.sem("dve_step"), nth())
        V.tensor_tensor(tile(OUT), tile(RW), tile(TAKEN), ALU.mult).then_inc(st.sem("dve_step"), 1)
        dve.wait_ge(st.sem("dve_step"), nth())
        V.tensor_tensor(tile(OUT), tile(OUT), spread(5), ALU.mult).then_inc(st.sem("dve_step"), 1)
        dve.wait_ge(st.sem("dve_step"), nth())


def moe_layer(nc, A, K, psum, x_in, x_out, weights, SLOTS):
    with ExitStack() as ctx:
        st = Stage(nc, ctx, "moe", psum, K["sems"])
        ident, tri, ones = K["ident"], K["tri"], K["ones"]
        gate, wg, wu, wd = weights["gate"], weights["egate"], weights["eup"], weights["edown"]
        SL = range(SLOTS)
        rank8 = st.sb("rank8", [NE])
        carry = st.sb("carry", [NE])
        bufs = []
        for s in SL:
            rt = st.sb(f"rt{s}", [24, NT, NE + 1])
            bufs.append({"x": st.sb(f"x{s}", [NT, D]), "xT": st.sb(f"xT{s}", [DC, T]), "acc": st.sb(f"acc{s}", [NT, D]),
                         "silu": st.sb(f"silu{s}", [2, T]), "h": st.sb(f"h{s}", [NE + SHF, T]),
                         "rt": rt, "mask": rt[:, 23, :, 0:NE], "per_token": st.sb(f"per_token{s}", [13, NT]),
                         "carry": carry, "norm": Norm(st, s)})

        with nc.Block() as block:
            @block.vector
            def _(dve):
                nc.vector.memset(carry[:], 0.0).then_inc(st.sem("zeroed"), 1)
                dve.wait_ge(st.sem("zeroed"), 1)

            @block.gpsimd
            def _(pool):
                nc.gpsimd.iota(rank8[:], pattern=[[-1, NE]], base=NE, channel_multiplier=0,
                               allow_small_or_imprecise_dtypes=True)

            @block.sync
            def _(sp):
                weights.arrive(sp)
        st.zero_sems()

        with nc.Fori(0, B // SLOTS) as turn:
            with nc.Block() as block:
                @block.tensor
                def _(pe):
                    for s in SL:
                        pe.wait_ge(st.sem(f"x_in{s}"), 16)
                        transposes(st, pe, f"xT{s}", bufs[s]["x"], ident[:])
                    for s in SL:
                        xT = bufs[s]["xT"]
                        pe.wait_ge(*st.emptied(f"xT{s}"))
                        o = st.claim(f"logits{s}")
                        for t in range(NT):
                            for c in range(DC):
                                last = nc.tensor.matmul(o[:, 0, 16 * t:16 * t + NE + 1], xT[:, c, t * P:t * P + P],
                                                        gate[:, c, :], start=c == 0, stop=c == DC - 1)
                        last.then_inc(st.filling(f"logits{s}"), 1)
                    for s in SL:
                        xT = bufs[s]["xT"]
                        for e in range(NE + SHF):
                            if e == 2:
                                pe.wait_ge(st.sem(f"mask{s}"), 1)
                                o = st.claim(f"count{s}")
                                for a, m in enumerate((tri, ones)):
                                    last = nc.tensor.matmul(f3(o[:, a, 0:32], NT), m[:], bufs[s]["mask"],
                                                            start=True, stop=True)
                                last.then_inc(st.filling(f"count{s}"), 1)
                            o = st.claim(f"gu{s}_{e}")
                            for a, w in enumerate((wg, wu)):
                                for c in range(DC):
                                    last = nc.tensor.matmul(o[:, a, :], w[:, c, e * P:e * P + P], xT[:, c, :],
                                                            start=c == 0, stop=c == DC - 1)
                            last.then_inc(st.filling(f"gu{s}_{e}"), 1)
                    for s in SL:
                        for e in range(NE + 1):
                            pe.wait_ge(*st.emptied(f"gu{s}_{e if e < NE else NE + SHF - 1}"))
                            token_major(st, f"down{s}_{e}", bufs[s]["h"], wd, kc=1 if e < NE else SHF, base=e)

                @block.sync
                def _(sp):
                    for s in SL:
                        sp.dma_start(bufs[s]["x"][:], tokens(x_in, turn * SLOTS + s)).then_inc(st.sem(f"x_in{s}"), 16)
                    for s in SL:
                        sp.wait_ge(st.sem(f"x_out{s}"), 1)
                        sp.dma_start(tokens(x_out, turn * SLOTS + s), bufs[s]["x"][:]).then_inc(st.sem("stored"), 16)
                    sp.wait_ge(st.sem("stored"), 16 * SLOTS)

                @block.scalar
                def _(act):
                    for s in SL:
                        copy_xT(st, act, f"xT{s}", bufs[s]["xT"])
                    for s in SL:
                        Z = bufs[s]
                        rt = Z["rt"]
                        act.wait_ge(st.sem(f"expo{s}"), 1)
                        ex = rt[:, 14:18, :, :].rearrange("p k t e -> p (k t) e")[:, :, 0:NE]
                        nc.scalar.activation(ex, ex, ACT.Exp).then_inc(st.sem(f"exped{s}"), 1)
                        for e in range(NE + SHF):
                            if e == 2:
                                act.wait_ge(st.sem(f"expo{s}"), 2)
                                nc.scalar.activation(rt[:, 21, :, :], rt[:, 21, :, :], ACT.Exp).then_inc(
                                    st.sem(f"exped{s}"), 1)
                            act.wait_ge(*st.full(f"gu{s}_{e}"))
                            o = st.region(f"gu{s}_{e}")
                            if e >= 2:
                                act.wait_ge(*st.emptied(f"gu{s}_{e - 2}"))
                            nc.scalar.activation(Z["silu"][:, e % 2, :], o[:, 0, :], ACT.Silu).then_inc(
                                st.sem(f"silu{s}"), 1)

                @block.vector
                def _(dve):
                    nth = counter()
                    V = nc.vector
                    for s in SL:
                        dve.wait_ge(*st.full(f"logits{s}"))
                        o = st.region(f"logits{s}")
                        V.tensor_copy(bufs[s]["rt"][:, 0, :, :], f3(o[:, 0, 0:64], NT)[:, :, 0:NE + 1]).then_inc(
                            st.emptying(f"logits{s}"), 1)
                    for s in SL:
                        Z = bufs[s]
                        route(nc, dve, nth, st, s, Z, rank8, 0)
                        for e in range(NE + SHF):
                            if e == 2:
                                route(nc, dve, nth, st, s, Z, rank8, 1)
                            dve.wait_ge(*st.full(f"gu{s}_{e}"))
                            o = st.region(f"gu{s}_{e}")
                            dve.wait_ge(st.sem(f"silu{s}"), e + 1)
                            V.tensor_tensor(Z["h"][:, e, :], Z["silu"][:, e % 2, :], o[:, 1, :],
                                            ALU.mult).then_inc(st.emptying(f"gu{s}_{e}"), 1)
                    for s in SL:
                        Z = bufs[s]
                        acc, w = Z["acc"], Z["rt"][:, 21, :, :]
                        for e in range(NE + 1):
                            dve.wait_ge(*st.full(f"down{s}_{e}"))
                            o = flat(st.region(f"down{s}_{e}")[:])
                            if e:
                                dve.wait_ge(*st.emptied(f"down{s}_{e - 1}"))
                            for t in range(NT):
                                last = V.scalar_tensor_tensor(acc[:, t, :], o[:, t * D:t * D + D], w[:, t, e:e + 1],
                                                              (acc if e else Z["x"])[:, t, :], ALU.mult, ALU.add)
                            last.then_inc(st.emptying(f"down{s}_{e}"), 1)
                        dve.wait_ge(*st.emptied(f"down{s}_{NE}"))
                        Z["norm"].vector(dve, nth, acc, Z["x"], f"x_out{s}")

                @block.gpsimd
                def _(pool):
                    nth = counter()
                    for s in SL:
                        bufs[s]["norm"].gpsimd(pool, nth, K["neg_half"], 1e-5)
            st.zero_sems()
def mamba_layer(nc, A, K, psum, x_in, x_out, weights, SLOTS):
    with ExitStack() as ctx:
        st = Stage(nc, ctx, "mamba", psum, K["sems"])
        ident, tri, ones = K["ident"], K["tri"], K["ones"]
        w_in, w_out = weights["in_proj"], weights["out_proj"]
        inner = MF * P
        X0, B0, DT0 = inner, 2 * inner, 2 * inner + 2 * MN
        x, normed, xT = st.sb("x", [NT, D]), st.sb("normed", [NT, D]), st.sb("xT", [DC, T])
        zs, xr, xh = st.sb("zs", [MF, T]), st.sb("xr", [MF, T + 4]), st.sb("xh", [MF, T])
        bct, bt, cbm = st.sb("bct", [2, T]), st.sb("bt", [NT, P]), st.sb("cbm", [NT, P])
        dtx, dtxd = st.sb("dtx", [NT, inner]), st.sb("dtxd", [NT, inner])
        inter, intra = st.sb("inter", [MH, T]), st.sb("intra", [MH, T])
        states = st.sb("states", [NT - 1, inner])
        dts, cs, csT = st.sb("dts", [4, NT * MH]), st.sb("cs", [NT * MH]), st.sb("csT", [T])
        dj, eend = st.sb("dj", [NT * MH]), st.sb("eend", [NT, MH])
        a_neg, sel8 = st.sb("a_neg", [MH]), st.sb("sel8", [MH, P])
        norm = Norm(st, 0)
        z_, abs_, dt, dtA = (dts[:, i, :] for i in range(4))

        with nc.Block() as block:
            @block.scalar
            def _(act):
                nc.scalar.activation(a_neg[:], K["A_log"], ACT.Exp).then_inc(st.sem("a_exp"), 1)

            @block.vector
            def _(dve):
                nc.vector.memset(xr[:, :, 0:4], 0.0)
                dve.wait_ge(st.sem("a_exp"), 1)
                nc.vector.tensor_scalar(a_neg[:], a_neg[:], -1.0, None, ALU.mult)

            @block.gpsimd
            def _(pool):
                nc.gpsimd.memset(sel8[:], 0.0).then_inc(st.sem("zeroed"), 1)
                pool.wait_ge(st.sem("zeroed"), 1)
                nc.gpsimd.affine_select(out=sel8[0:MH], in_=sel8[0:MH], compare_op=ALU.not_equal, fill=1.0, base=0,
                                        pattern=[[-1, MH], [0, P]], channel_multiplier=1)

            @block.sync
            def _(sp):
                weights.arrive(sp)
        st.zero_sems()

        with nc.Fori(0, B // SLOTS) as turn:
            with nc.Block() as block:
                @block.tensor
                def _(pe):
                    mm, tr = nc.tensor.matmul, nc.tensor.transpose
                    pe.wait_ge(st.sem("normed"), 1)
                    transposes(st, pe, "xT", normed, ident[:])
                    pe.wait_ge(*st.emptied("xT"))
                    o = st.claim("b_dt")
                    for t in range(NT):
                        for dst, c0, n in ((o[:, 0, t * P:t * P + P], B0, P), (o[:, 1, t * MH:t * MH + MH], DT0, MH)):
                            for c in range(DC):
                                last = mm(dst, xT[:, c, t * P:t * P + P], w_in[:, c, c0:c0 + n],
                                          start=c == 0, stop=c == DC - 1)
                    last.then_inc(st.filling("b_dt"), 1)
                    feature_major(st, "xs0", w_in, X0, xT)
                    feature_major(st, "xs1", w_in, X0 + 2 * P, xT)
                    feature_major(st, "bcT", w_in, B0, xT)
                    feature_major(st, "z0", w_in, 0, xT)
                    feature_major(st, "z1", w_in, 2 * P, xT)
                    pe.wait_ge(st.sem("dtA"), 1)
                    o = st.claim("cs")
                    mm(o[:, 0, 0:NT * MH], tri[:], dtA, start=True, stop=True)
                    mm(o[:, 1, 0:NT * MH], ones[:], dtA, start=True, stop=True).then_inc(st.filling("cs"), 1)
                    pe.wait_ge(*st.emptied("bcT"))
                    o = st.claim("cb")
                    for t in range(NT):
                        last = mm(o[:, 0, t * P:t * P + P], bct[:, 0, t * P:t * P + P], bct[:, 1, t * P:t * P + P],
                                  start=True, stop=True)
                    last.then_inc(st.filling("cb"), 1)
                    pe.wait_ge(*st.emptied("cs"))
                    o = st.claim("csT")
                    for t in range(NT):
                        last = tr(o[0:MH, 0, t * P:t * P + P], cs[:, t * MH:t * MH + MH], ident[:])
                    last.then_inc(st.filling("csT"), 1)
                    pe.wait_ge(st.sem("conv_out"), MF)
                    for i in range(2):
                        o = st.claim(f"x_tok{i}")
                        for a in range(2):
                            t = 2 * i + a
                            for f in range(MF):
                                last = tr(o[:, a, f * P:f * P + P], xh[:, f, t * P:t * P + P], ident[:])
                        last.then_inc(st.filling(f"x_tok{i}"), 1)
                    pe.wait_ge(*st.emptied("csT"))
                    for hp in range(MH // 2):
                        o = st.claim(f"spread{hp}")
                        for a in range(2):
                            last = mm(o[:, a, :], sel8[0:MH, 2 * hp + a, :], csT[0:MH, :], start=True, stop=True)
                        last.then_inc(st.filling(f"spread{hp}"), 1)
                    pe.wait_ge(st.sem("dtxd"), 1)
                    for t in range(NT - 1):
                        o = st.claim(f"add{t}")
                        mm(o[:, 0, :], bt[:, t, :], dtxd[:, t, :], start=True, stop=True).then_inc(
                            st.filling(f"add{t}"), 1)
                    pe.wait_ge(*st.emptied(f"add{NT - 2}"))
                    for i in range(2):
                        o = st.claim(f"y{i}")
                        for a in range(2):
                            f = 2 * i + a
                            pe.wait_ge(st.sem("intra"), f + 1)
                            pe.wait_ge(st.sem("inter"), f + 1)
                            for t in range(NT):
                                for r in range(2):
                                    h = 2 * f + r
                                    dst = o[64 * r:64 * r + 64, a, t * P:t * P + P]
                                    if t:
                                        mm(dst, states[:, t - 1, 64 * h:64 * h + 64], inter[:, h, t * P:t * P + P],
                                           start=True, stop=False)
                                    last = mm(dst, dtx[:, t, 64 * h:64 * h + 64], intra[:, h, t * P:t * P + P],
                                              start=t == 0, stop=True)
                        last.then_inc(st.filling(f"y{i}"), 1)
                    pe.wait_ge(st.sem("gated"), 2)
                    token_major(st, "out", zs, w_out, kc=MF)

                @block.sync
                def _(sp):
                    sp.dma_start(x[:], tokens(x_in, turn)).then_inc(st.sem("x_in"), 16)
                    sp.wait_ge(st.sem("x_out"), 1)
                    sp.dma_start(tokens(x_out, turn), x[:]).then_inc(st.sem("stored"), 16)
                    sp.wait_ge(st.sem("stored"), 16)

                @block.scalar
                def _(act):
                    A_ = nc.scalar.activation
                    copy_xT(st, act, "xT", xT, K["norm_w"])
                    act.wait_ge(st.sem("dt_in"), 1)
                    A_(abs_, abs_, ACT.Exp).then_inc(st.sem("act_step"), 1)
                    act.wait_ge(st.sem("act_step"), 1)
                    A_(abs_, abs_, ACT.Ln, bias=1.0).then_inc(st.sem("dt_log"), 1)
                    for f in range(MF):
                        if f % 2 == 0:
                            act.wait_ge(*st.emptied(f"xs{f // 2}"))
                        A_(xh[:, f, :], xr[:, f, 4:T + 4], ACT.Identity, scale=K["conv_w"][:, f, 3:4],
                           bias=K["conv_b"][:, f:f + 1]).then_inc(st.sem("conv_start"), 1)
                    act.wait_ge(*st.full("bcT"))
                    o = st.region("bcT")
                    A_(bct[:], o[:], ACT.Copy).then_inc(st.emptying("bcT"), 1)
                    for i in range(2):
                        act.wait_ge(*st.full(f"z{i}"))
                        o = st.region(f"z{i}")
                        A_(zs[:, 2 * i:2 * i + 2, :], o[:], ACT.Silu).then_inc(st.emptying(f"z{i}"), 1)
                    for f in range(MF):
                        act.wait_ge(st.sem("conv_taps"), f + 1)
                        A_(xh[:, f, :], xh[:, f, :], ACT.Silu).then_inc(st.sem("conv_out"), 1)
                    act.wait_ge(*st.full("csT"))
                    o = st.region("csT")
                    A_(csT[0:MH, :], o[0:MH, 0, :], ACT.Copy).then_inc(st.emptying("csT"), 1)
                    act.wait_ge(st.sem("dj_in"), 1)
                    A_(dj[:], dj[:], ACT.Exp).then_inc(st.sem("dj_out"), 1)
                    for hp in range(MH // 2):
                        two = slice(2 * hp, 2 * hp + 2)
                        act.wait_ge(st.sem("differences"), hp + 1)
                        A_(inter[:, two, :], psum[st.place[f"spread{hp}"][0]][:], ACT.Exp).then_inc(
                            st.emptying(f"spread{hp}"), 1)
                        A_(intra[:, two, :], intra[:, two, :], ACT.Exp).then_inc(st.sem("decay"), 1)

                @block.vector
                def _(dve):
                    V = nc.vector
                    nth = counter()
                    dve.wait_ge(st.sem("x_in"), 16)
                    norm.vector(dve, nth, x, normed, "normed", rms=True)
                    dve.wait_ge(*st.full("b_dt"))
                    o = st.region("b_dt")
                    V.tensor_tensor(f3(z_, NT), f3(o[:, 1, 0:NT * MH], NT), times(K["dt_bias"], NT), ALU.add).then_inc(
                        st.sem("dve_step"), 1)
                    dve.wait_ge(st.sem("dve_step"), nth())
                    V.scalar_tensor_tensor(abs_, z_, -1.0, z_, ALU.mult, ALU.min).then_inc(st.sem("dt_in"), 1)
                    V.tensor_copy(flat(bt[:]), o[:, 0, :]).then_inc(st.emptying("b_dt"), 1)
                    for i in range(2):
                        dve.wait_ge(*st.full(f"xs{i}"))
                        o = st.region(f"xs{i}")
                        V.tensor_copy(xr[:, 2 * i:2 * i + 2, 4:T + 4], o[:]).then_inc(st.emptying(f"xs{i}"), 1)
                    dve.wait_ge(st.sem("dt_log"), 1)
                    V.scalar_tensor_tensor(dt, z_, 0.0, abs_, ALU.max, ALU.add).then_inc(st.sem("dve_step"), 1)
                    dve.wait_ge(st.sem("dve_step"), nth())
                    V.tensor_tensor(f3(dtA, NT), f3(dt, NT), times(a_neg[:], NT), ALU.mult).then_inc(st.sem("dtA"), 1)
                    for f in range(MF):
                        dve.wait_ge(st.sem("conv_start"), f + 1)
                        for k in range(3):
                            ins = V.scalar_tensor_tensor(xh[:, f, :], xr[:, f, 1 + k:1 + k + T],
                                                         K["conv_w"][:, f, k:k + 1], xh[:, f, :], ALU.mult, ALU.add)
                            if k < 2:
                                ins.then_inc(st.sem("dve_step"), 1)
                                dve.wait_ge(st.sem("dve_step"), nth())
                            else:
                                ins.then_inc(st.sem("conv_taps"), 1)
                    dve.wait_ge(*st.full("cs"))
                    o = st.region("cs")
                    V.tensor_copy(cs[:], o[:, 0, 0:NT * MH]).then_inc(st.sem("dve_step"), 1)
                    dve.wait_ge(st.sem("dve_step"), nth())
                    V.tensor_tensor(dj[:], o[:, 1, 0:NT * MH], cs[:], ALU.subtract).then_inc(st.emptying("cs"), 1)
                    dve.wait_ge(*st.emptied("cs"))
                    V.tensor_scalar(dj[:], dj[:], 0.0, None, ALU.min).then_inc(st.sem("dj_in"), 1)
                    dve.wait_ge(*st.full("cb"))
                    o = st.region("cb")
                    V.tensor_tensor(cbm[:], f3(o[:, 0, :], NT), times(tri[:], NT), ALU.mult).then_inc(
                        st.emptying("cb"), 1)
                    for i in range(2):
                        dve.wait_ge(*st.full(f"x_tok{i}"))
                        o = st.region(f"x_tok{i}")
                        for a in range(2):
                            t = 2 * i + a
                            last = V.tensor_tensor(f3(dtx[:, t, :], MH), f3(o[:, a, :], MH),
                                                   over(dt[:, t * MH:t * MH + MH], 64), ALU.mult)
                        last.then_inc(st.emptying(f"x_tok{i}"), 1)
                    dve.wait_ge(*st.emptied("x_tok1"))
                    dve.wait_ge(st.sem("dj_out"), 1)
                    for t in range(NT - 1):
                        last = V.tensor_tensor(f3(dtxd[:, t, :], MH), f3(dtx[:, t, :], MH),
                                               over(dj[:, t * MH:t * MH + MH], 64), ALU.mult)
                    last.then_inc(st.sem("dtxd"), 1)
                    for hp in range(MH // 2):
                        dve.wait_ge(*st.full(f"spread{hp}"))
                        o = st.region(f"spread{hp}")
                        for a in range(2):
                            h = 2 * hp + a
                            for t in range(NT):
                                last = V.tensor_scalar(intra[:, h, t * P:t * P + P], o[:, a, t * P:t * P + P],
                                                       cs[:, t * MH + h:t * MH + h + 1], 0.0, ALU.subtract, ALU.min)
                        last.then_inc(st.sem("differences"), 1)
                    dve.wait_ge(st.sem("tile_decay"), MH // 2)
                    for t in range(NT - 1):
                        dve.wait_ge(*st.full(f"add{t}"))
                        o = st.region(f"add{t}")
                        if t:
                            dve.wait_ge(*st.emptied(f"add{t - 1}"))
                            V.tensor_tensor(f3(states[:, t, :], MH), f3(states[:, t - 1, :], MH),
                                            over(eend[:, t, :], 64), ALU.mult).then_inc(st.sem("dve_step"), 1)
                            dve.wait_ge(st.sem("dve_step"), nth())
                            ins = V.tensor_tensor(states[:, t, :], states[:, t, :], o[:, 0, :], ALU.add)
                        else:
                            ins = V.tensor_copy(states[:, 0, :], o[:, 0, :])
                        ins.then_inc(st.emptying(f"add{t}"), 1)
                    for f in range(MF):
                        dve.wait_ge(st.sem("decay"), f + 1)
                        two = slice(2 * f, 2 * f + 2)
                        for h in (2 * f, 2 * f + 1):
                            last = V.tensor_tensor(intra[:, h, :], intra[:, h, :], flat(cbm[:]), ALU.mult)
                        last.then_inc(st.sem("intra"), 1)
                    for i in range(2):
                        dve.wait_ge(*st.full(f"y{i}"))
                        o = st.region(f"y{i}")
                        for a in range(2):
                            f = 2 * i + a
                            last = V.scalar_tensor_tensor(xh[:, f, :], xh[:, f, :], K["mD"][:, f:f + 1], o[:, a, :],
                                                          ALU.mult, ALU.add)
                        last.then_inc(st.emptying(f"y{i}"), 1)
                        dve.wait_ge(*st.emptied(f"y{i}"))
                        V.tensor_tensor(zs[:, 2 * i:2 * i + 2, :], zs[:, 2 * i:2 * i + 2, :],
                                        xh[:, 2 * i:2 * i + 2, :], ALU.mult).then_inc(st.sem("gated"), 1)
                    dve.wait_ge(*st.full("out"))
                    o = st.region("out")
                    V.scalar_tensor_tensor(flat(x[:]), flat(x[:]), 2.0, flat(o[:]), ALU.mult, ALU.add).then_inc(
                        st.emptying("out"), 1)
                    dve.wait_ge(*st.emptied("out"))
                    norm.vector(dve, nth, x, x, "x_out")

                @block.gpsimd
                def _(pool):
                    G = nc.gpsimd
                    nth = counter()
                    norm.gpsimd(pool, nth, K["neg_half"], 1e-6)
                    for hp in range(MH // 2):
                        two = slice(2 * hp, 2 * hp + 2)
                        pool.wait_ge(*st.emptied(f"spread{hp}"))
                        ends = inter[:, two, :].rearrange("p h (t n) -> p t h n", t=NT)[:, :, :, P - 1]
                        ins = G.tensor_copy(eend[:, :, two], ends)
                        ins.then_inc(st.sem("tile_decay"), 1)
                        pool.wait_ge(st.sem("tile_decay"), hp + 1)
                        for h in (2 * hp, 2 * hp + 1):
                            last = G.tensor_tensor(inter[:, h, :], inter[:, h, :], bct[:, 1, :], ALU.mult)
                        last.then_inc(st.sem("inter"), 1)
                    norm.gpsimd(pool, nth, K["neg_half"], 1e-5)
            st.zero_sems()
def psi_layer(nc, A, K, psum, x_in, x_out, weights, SLOTS):
    with ExitStack() as ctx:
        st = Stage(nc, ctx, "psi", psum, K["sems"])
        ident = K["ident"]
        wq, wo = weights["pWq"], weights["pWo"]
        G2, GQ = 2 * NT * GH, NT * GH
        x, xT, QT = st.sb("x", [NT, D]), st.sb("xT", [DC, T]), st.sb("QT", [DC, T])
        ctxT, ctxv, oT = st.sb("ctxT", [DC, T]), st.sb("ctxv", [NT, D]), st.sb("oT", [DC, T])
        proj, proj_b = st.sb("proj", [DC, 24 * GH]), st.sb("proj_b", [24 * GH])
        gen, theta = st.sb("gen", [G2, 24]), st.sb("theta", [G2, 8])
        turns, angle = st.sb("turns", [2, G2 * 8]), st.sb("angle", [2, G2 * 8])
        growth, tmp = st.sb("growth", [G2, 8]), st.sb("tmp", [G2, 8])
        re, im = st.sb("re", [G2, 12]), st.sb("im", [G2, 12])
        prods = [st.sb(f"prod{i}", [G2, 4, 8]) for i in range(4)]
        n2 = st.sb("n2", [2, G2])
        feat, fT = st.sb("feat", [G2, P]), st.sb("fT", [GH, 3, T])
        scores, wedge = st.sb("scores", [GQ, T]), st.sb("wedge", [2, T])
        pT = fT[:].rearrange("p h a n -> p (h a) n")[:, 0:2 * NT, :].rearrange("p (a j) n -> p a j n", a=2)
        mx, sums = st.sb("mx", [GQ]), st.sb("sums", [GQ])
        key_w, key_l = st.sb("key_w", [1]), st.sb("key_l", [1])
        geo, neg_g2 = st.sb("geo", [4]), st.sb("neg_g2", [1])
        norm = Norm(st, 0)

        with nc.Block() as block:
            @block.vector
            def _(dve):
                nth = counter()
                V = nc.vector
                V.memset(feat[:], 0.0)
                V.memset(proj[:], 0.0).then_inc(st.sem("zeroed"), 1)
                V.reciprocal(mx[:, 0:1], K["temperature"]).then_inc(st.sem("dve_step"), 1)
                dve.wait_ge(st.sem("dve_step"), nth())
                V.tensor_scalar(geo[:], K["geo_w"], mx[:, 0:1], 0.25, ALU.mult, ALU.mult).then_inc(
                    st.sem("dve_step"), 1)
                dve.wait_ge(st.sem("dve_step"), nth())
                V.tensor_scalar(neg_g2[:], geo[:, 2:3], -1.0, None, ALU.mult)

            @block.gpsimd
            def _(pool):
                nth = counter()
                nc.gpsimd.memset(key_w[:], 0.0).then_inc(st.sem("pool_step"), 1)
                pool.wait_ge(st.sem("pool_step"), nth())
                for upto, v in ((72, -1.0), (64, -2.0), (40, -1.0), (32, -2.0), (8, 1.0)):
                    nc.gpsimd.affine_select(out=key_w[:], in_=key_w[:], compare_op=ALU.is_ge, fill=v, base=-upto,
                                            pattern=[[0, 1]], channel_multiplier=1).then_inc(st.sem("pool_step"), 1)
                    pool.wait_ge(st.sem("pool_step"), nth())
                nc.gpsimd.memset(key_l[:], 0.0).then_inc(st.sem("pool_step"), 1)
                pool.wait_ge(st.sem("pool_step"), nth())
                nc.gpsimd.memset(key_l[LIN:P, :], 1.0)

            @block.sync
            def _(sp):
                sp.wait_ge(st.sem("zeroed"), 1)
                with nc.allow_non_contiguous_dma("small arrays, once"):
                    for h in range(GH):
                        sp.dma_start(proj[64 * (h % 2):64 * (h % 2) + 64, h // 2, 24 * h:24 * h + 24],
                                     A["proj_w"]).then_inc(st.sem("proj_in"), 16)
                        sp.dma_start(proj_b[:, 24 * h:24 * h + 24],
                                     A["proj_b"].rearrange("(a n) -> a n", a=1).broadcast_to([P, 24])).then_inc(
                                         st.sem("proj_in"), 16)
                sp.wait_ge(st.sem("proj_in"), 32 * GH)
                weights.arrive(sp)
        st.zero_sems()

        with nc.Fori(0, B // SLOTS) as turn:
            with nc.Block() as block:
                @block.tensor
                def _(pe):
                    mm, tr = nc.tensor.matmul, nc.tensor.transpose
                    pe.wait_ge(st.sem("x_in"), 16)
                    transposes(st, pe, "xT", x, ident[:])
                    pe.wait_ge(*st.emptied("xT"))
                    feature_major(st, "Q", wq, 0, xT)
                    pe.wait_ge(*st.emptied("Q"))
                    pe.wait_ge(st.sem("ctx_in"), 32)
                    o = st.claim("gen")
                    for a, src in enumerate((QT, ctxT)):
                        for t in range(NT):
                            for c in range(DC):
                                last = mm(o[:, a, 96 * t:96 * t + 96], src[:, c, t * P:t * P + P], proj[:, c, :],
                                          start=c == 0, stop=c == DC - 1)
                    last.then_inc(st.filling("gen"), 1)
                    pe.wait_ge(st.sem("feat_re"), 1)
                    pe.wait_ge(st.sem("feat_im"), 1)
                    for h in range(GH):
                        o = st.claim(f"fT{h}")
                        for a in range(2):
                            for t in range(NT):
                                last = tr(o[:, a, t * P:t * P + P], feat[:, a * GQ + t * GH + h, :], ident[:])
                        last.then_inc(st.filling(f"fT{h}"), 1)
                    for h in range(GH):
                        pe.wait_ge(*st.emptied(f"fT{h}"))
                        for t in range(NT):
                            o = st.claim(f"s{h}_{t}")
                            for a in range(2):
                                last = mm(o[:, a, :], fT[:, h, 0, t * P:t * P + P], fT[:, h, 1 + a, :],
                                          start=True, stop=True)
                            last.then_inc(st.filling(f"s{h}_{t}"), 1)
                    po = st.claim("po", long=True)
                    for h in range(GH):
                        pe.wait_ge(st.sem("probs"), h + 1)
                        for i in range(NT // 2):
                            o = st.claim(f"pT{h}_{i}")
                            for a in range(2):
                                j = 2 * i + a
                                for t in range(NT):
                                    last = tr(o[:, a, t * P:t * P + P], scores[:, h * NT + t, j * P:j * P + P], ident[:])
                            last.then_inc(st.filling(f"pT{h}_{i}"), 1)
                        pe.wait_ge(*st.emptied(f"pT{h}_0"))
                        pe.wait_ge(*st.emptied(f"pT{h}_1"))
                        r = 64 * (h % 2)
                        for j in range(NT):
                            last = mm(po[r:r + 64, h // 2, :], ctxv[:, j, 64 * h:64 * h + 64], pT[:, h % 2, j, :],
                                      start=j == 0, stop=j == NT - 1)
                    last.then_inc(st.filling("po"), 1)
                    pe.wait_ge(*st.emptied("po"))
                    token_major(st, "out", oT, wo)

                @block.sync
                def _(sp):
                    sp.dma_start(x[:], tokens(x_in, turn)).then_inc(st.sem("x_in"), 16)
                    sp.dma_start(ctxT[:], features(A["ctxT"], turn)).then_inc(st.sem("ctx_in"), 16)
                    sp.dma_start(ctxv[:], tokens(A["ctx"], turn)).then_inc(st.sem("ctx_in"), 16)
                    sp.wait_ge(st.sem("x_out"), 1)
                    sp.dma_start(tokens(x_out, turn), x[:]).then_inc(st.sem("stored"), 16)
                    sp.wait_ge(st.sem("stored"), 16)

                @block.scalar
                def _(act):
                    A_ = nc.scalar.activation
                    copy_xT(st, act, "xT", xT)
                    copy_xT(st, act, "Q", QT, K["ones"], K["pWq_b"])
                    act.wait_ge(st.sem("theta"), 1)
                    A_(growth[:], theta[:], ACT.Exp).then_inc(st.sem("exp_theta"), 1)
                    act.wait_ge(st.sem("angle"), 1)
                    A_(angle[:], angle[:], ACT.Sin).then_inc(st.sem("sines"), 1)
                    act.wait_ge(st.sem("n2"), 1)
                    A_(n2[:, 1, :], n2[:, 0, :], ACT.Sqrt, bias=K["eps6"][:]).then_inc(st.sem("norms"), 1)
                    for h in range(GH):
                        act.wait_ge(*st.full(f"fT{h}"))
                        o = st.region(f"fT{h}")
                        A_(fT[:, h, 0, :], o[:, 0, :], ACT.Copy)
                        A_(fT[:, h, 1, :], o[:, 1, :], ACT.Copy, scale=key_w[:])
                        A_(fT[:, h, 2, :], o[:, 1, :], ACT.Copy, scale=key_l[:]).then_inc(st.emptying(f"fT{h}"), 1)
                    for i in range(GQ):
                        act.wait_ge(st.sem("wedge_in"), i + 1)
                        A_(wedge[:, i % 2, :], wedge[:, i % 2, :], ACT.Sqrt, bias=K["eps6"][:]).then_inc(
                            st.sem("wedge_root"), 1)
                    act.wait_ge(st.sem("maxima"), 1)
                    for i in range(GQ):
                        A_(scores[:, i, :], scores[:, i, :], ACT.Exp, bias=mx[:, i:i + 1],
                           accum_out=sums[:, i:i + 1]).then_inc(st.sem("exped"), 1)
                    for h in range(GH):
                        for i in range(2):
                            act.wait_ge(*st.full(f"pT{h}_{i}"))
                            o = st.region(f"pT{h}_{i}")
                            A_(pT[:, h % 2, 2 * i:2 * i + 2, :], o[:], ACT.Copy).then_inc(
                                st.emptying(f"pT{h}_{i}"), 1)
                    act.wait_ge(*st.full("po"))
                    o = st.region("po")
                    A_(oT[:], o[:], ACT.Copy).then_inc(st.emptying("po"), 1)

                @block.vector
                def _(dve):
                    V = nc.vector
                    TT, TS, STT = V.tensor_tensor, V.tensor_scalar, V.scalar_tensor_tensor
                    nth = counter()
                    dve.wait_ge(*st.full("gen"))
                    o = st.region("gen")
                    for a in range(2):
                        last = TT(gen[:, a * GQ:a * GQ + GQ, :].rearrange("p (t h) n -> p t (h n)", t=NT),
                                  f3(o[:, a, 0:96 * NT], NT), times(proj_b[:], NT), ALU.add)
                    last.then_inc(st.emptying("gen"), 1)
                    dve.wait_ge(*st.emptied("gen"))
                    TS(theta[:], gen[:, :, 16:24], -8.0, 8.0, ALU.max, ALU.min).then_inc(st.sem("theta"), 1)
                    dve.wait_ge(st.sem("theta"), 1)
                    th = theta[:].rearrange("p g n -> p (g n)")
                    TS(turns[:, 0, :], th, 1 / (2 * PI), None, ALU.mult)
                    TS(turns[:, 1, :], th, 1 / (2 * PI), 0.25, ALU.mult, ALU.add).then_inc(st.sem("dve_step"), 1)
                    dve.wait_ge(st.sem("dve_step"), nth())
                    TS(turns[:], turns[:], ROUND, None, ALU.add).then_inc(st.sem("dve_step"), 1)
                    dve.wait_ge(st.sem("dve_step"), nth())
                    TS(turns[:], turns[:], -ROUND, None, ALU.add).then_inc(st.sem("dve_step"), 1)
                    dve.wait_ge(st.sem("dve_step"), nth())
                    for a in range(2):
                        last = STT(angle[:, a, :], turns[:, a, :], -TURN_HI, th, ALU.mult, ALU.add)
                    last.then_inc(st.sem("dve_step"), 1)
                    dve.wait_ge(st.sem("dve_step"), nth())
                    STT(angle[:], turns[:], -TURN_LO, angle[:], ALU.mult, ALU.add).then_inc(st.sem("dve_step"), 1)
                    dve.wait_ge(st.sem("dve_step"), nth())
                    TS(angle[:, 1, :], angle[:, 1, :], PI / 2, None, ALU.add).then_inc(st.sem("dve_step"), 1)
                    dve.wait_ge(st.sem("dve_step"), nth())
                    TS(angle[:], angle[:], -PI, PI, ALU.max, ALU.min).then_inc(st.sem("angle"), 1)
                    amp, bg = gen[:, :, 0:8], gen[:, :, 8:16]
                    sin, cos = (angle[:, a, :].rearrange("p (g n) -> p g n", g=G2) for a in range(2))
                    r, m = re[:, :, 0:8], im[:, :, 0:8]
                    dve.wait_ge(st.sem("exp_theta"), 1)
                    TT(tmp[:], amp, growth[:], ALU.mult).then_inc(st.sem("dve_step"), 1)
                    dve.wait_ge(st.sem("dve_step"), nth())
                    dve.wait_ge(st.sem("sines"), 1)
                    TT(m, bg, sin, ALU.mult)
                    TT(r, bg, cos, ALU.mult).then_inc(st.sem("dve_step"), 1)
                    dve.wait_ge(st.sem("dve_step"), nth())
                    TT(r, r, tmp[:], ALU.add).then_inc(st.sem("dve_step"), 1)
                    dve.wait_ge(st.sem("dve_step"), nth())
                    V.tensor_copy(re[:, :, 8:12], re[:, :, 0:4])
                    V.tensor_copy(im[:, :, 8:12], im[:, :, 0:4]).then_inc(st.sem("psi"), 1)
                    dve.wait_ge(st.sem("psi"), 1)
                    zz = feat[:, :, 0:8]
                    TT(tmp[:], r, r, ALU.mult)
                    TT(zz, m, m, ALU.mult).then_inc(st.sem("dve_step"), 1)
                    dve.wait_ge(st.sem("dve_step"), nth())
                    TT(zz, zz, tmp[:], ALU.add).then_inc(st.sem("dve_step"), 1)
                    dve.wait_ge(st.sem("dve_step"), nth())
                    V.tensor_reduce(n2[:, 0, :], zz, AX, ALU.add).then_inc(st.sem("n2"), 1)
                    for d in range(1, 5):
                        TT(prods[0][:, :, d - 1, :], r, re[:, :, d:d + 8], ALU.mult)
                        last = TT(prods[1][:, :, d - 1, :], m, im[:, :, d:d + 8], ALU.mult)
                    last.then_inc(st.sem("dve_step"), 1)
                    dve.wait_ge(st.sem("dve_step"), nth())
                    dve.wait_ge(st.sem("n2"), 1)
                    TT(zz[:, GQ:, :], over(n2[:, 0, GQ:], 8), zz[:, GQ:, :], ALU.subtract)
                    TT(feat[:, :, 8:40], prods[0][:].rearrange("p g d a -> p g (d a)"),
                       prods[1][:].rearrange("p g d a -> p g (d a)"), ALU.add)
                    V.tensor_copy(feat[:, 0:GQ, LIN:LIN + 8], r[:, 0:GQ, :])
                    V.tensor_copy(feat[:, 0:GQ, LIN + 8:LIN + 16], m[:, 0:GQ, :])
                    rk, mk = r[:, GQ:, :], m[:, GQ:, :]
                    TS(tmp[:, 0:GQ, :], rk, geo[:, 1:2], None, ALU.mult)
                    TS(tmp[:, GQ:, :], mk, geo[:, 1:2], None, ALU.mult).then_inc(st.sem("dve_step"), 1)
                    dve.wait_ge(st.sem("dve_step"), nth())
                    STT(feat[:, GQ:, LIN:LIN + 8], mk, geo[:, 2:3], tmp[:, 0:GQ, :], ALU.mult, ALU.add)
                    STT(feat[:, GQ:, LIN + 8:LIN + 16], rk, neg_g2[:], tmp[:, GQ:, :], ALU.mult, ALU.add)
                    dve.wait_ge(st.sem("norms"), 1)
                    V.tensor_copy(feat[:, 0:GQ, LIN + 16:LIN + 17], n2[:, 1, 0:GQ].unsqueeze(2))
                    TS(feat[:, GQ:, LIN + 16:LIN + 17], n2[:, 1, GQ:].unsqueeze(2), geo[:, 3:4], None,
                       ALU.mult).then_inc(st.sem("feat_re"), 1)
                    for i in range(GQ + 2):
                        if i >= 2:
                            dve.wait_ge(*st.emptied(f"s{(i - 2) // NT}_{(i - 2) % NT}"))
                        if i < GQ:
                            dve.wait_ge(*st.full(f"s{i // NT}_{i % NT}"))
                            o = st.region(f"s{i // NT}_{i % NT}")
                            TS(wedge[:, i % 2, :], o[:, 0, :], 0.0, None, ALU.max).then_inc(st.sem("wedge_in"), 1)
                        if 1 <= i <= GQ:
                            k = i - 1
                            name = f"s{k // NT}_{k % NT}"
                            dve.wait_ge(st.sem("wedge_root"), k + 1)
                            STT(scores[:, k, :], wedge[:, k % 2, :], geo[:, 0:1],
                                psum[st.place[name][0]][:, 1, :], ALU.mult, ALU.add).then_inc(st.emptying(name), 1)
                        if i >= 2:
                            k = i - 2
                            last = V.tensor_reduce(mx[:, k:k + 1], scores[:, k, :], AX, ALU.max)
                    last.then_inc(st.sem("dve_step"), 1)
                    dve.wait_ge(st.sem("dve_step"), nth())
                    TS(mx[:], mx[:], -1.0, None, ALU.mult).then_inc(st.sem("maxima"), 1)
                    for h in range(GH):
                        dve.wait_ge(st.sem("exped"), NT * h + NT)
                        four = slice(NT * h, NT * h + NT)
                        V.reciprocal(sums[:, four], sums[:, four]).then_inc(st.sem("dve_step"), 1)
                        dve.wait_ge(st.sem("dve_step"), nth())
                        for i in range(NT * h, NT * h + NT):
                            last = TS(scores[:, i, :], scores[:, i, :], sums[:, i:i + 1], None, ALU.mult)
                        last.then_inc(st.sem("probs"), 1)
                    TT(x[:], x[:], times(K["pWo_b"], NT), ALU.add).then_inc(st.sem("dve_step"), 1)
                    dve.wait_ge(st.sem("dve_step"), nth())
                    dve.wait_ge(*st.full("out"))
                    o = st.region("out")
                    TT(flat(x[:]), flat(x[:]), flat(o[:]), ALU.add).then_inc(st.emptying("out"), 1)
                    dve.wait_ge(*st.emptied("out"))
                    norm.vector(dve, nth, x, x, "x_out")

                @block.gpsimd
                def _(pool):
                    G = nc.gpsimd
                    nth = counter()
                    r, m = re[:, :, 0:8], im[:, :, 0:8]
                    pool.wait_ge(st.sem("psi"), 1)
                    for d in range(1, 5):
                        G.tensor_tensor(prods[2][:, :, d - 1, :], m, re[:, :, d:d + 8], ALU.mult)
                        last = G.tensor_tensor(prods[3][:, :, d - 1, :], r, im[:, :, d:d + 8], ALU.mult)
                    last.then_inc(st.sem("pool_step"), 1)
                    pool.wait_ge(st.sem("pool_step"), nth())
                    G.tensor_tensor(feat[:, :, 40:72], prods[2][:].rearrange("p g d a -> p g (d a)"),
                                    prods[3][:].rearrange("p g d a -> p g (d a)"), ALU.subtract).then_inc(
                                        st.sem("feat_im"), 1)
                    norm.gpsimd(pool, nth, K["neg_half"], 1e-5)
            st.zero_sems()
def ffn_layer(nc, A, K, psum, x_in, x_out, weights, SLOTS):
    with ExitStack() as ctx:
        st = Stage(nc, ctx, "ffn", psum, K["sems"])
        ident = K["ident"]
        SL = range(SLOTS)
        bufs = [{"x": st.sb(f"x{s}", [NT, D]), "xT": st.sb(f"xT{s}", [DC, T]), "silu": st.sb(f"silu{s}", [2, T]),
                 "h": st.sb(f"h{s}", [HF, T]), "norm": Norm(st, s)} for s in SL]
        wide = {n: st.sb(n, list(weights[n].shape[1:])) for n in ("w_gate", "w_up", "w_down")}

        with nc.Block() as block:
            @block.vector
            def _(dve):
                nth = counter()
                weights.arrive(dve)
                for n, w in wide.items():
                    nc.vector.tensor_copy(w[:], weights[n].bitcast(I32)).then_inc(st.sem("dequantized"), 1)
                    dve.wait_ge(st.sem("dequantized"), nth())
                    nc.vector.tensor_scalar(w[:], w[:], 1.0 / 127.0, None, ALU.mult).then_inc(
                        st.sem("dequantized"), 1)
                    dve.wait_ge(st.sem("dequantized"), nth())
        st.zero_sems()

        with nc.Fori(0, B // SLOTS) as turn:
            with nc.Block() as block:
                @block.tensor
                def _(pe):
                    for s in SL:
                        pe.wait_ge(st.sem(f"x_in{s}"), 16)
                        transposes(st, pe, f"xT{s}", bufs[s]["x"], ident[:])
                    for s in SL:
                        pe.wait_ge(*st.emptied(f"xT{s}"))
                        for e in range(HF):
                            o = st.claim(f"gu{s}_{e}")
                            for a, w in enumerate((wide["w_gate"], wide["w_up"])):
                                for c in range(DC):
                                    last = nc.tensor.matmul(o[:, a, :], w[:, c, e * P:e * P + P],
                                                            bufs[s]["xT"][:, c, :], start=c == 0, stop=c == DC - 1)
                            last.then_inc(st.filling(f"gu{s}_{e}"), 1)
                    for s in SL:
                        pe.wait_ge(*st.emptied(f"gu{s}_{HF - 3}"))
                        pe.wait_ge(*st.emptied(f"gu{s}_{HF - 2}"))
                        pe.wait_ge(*st.emptied(f"gu{s}_{HF - 1}"))
                        token_major(st, f"down{s}", bufs[s]["h"], wide["w_down"], kc=HF)

                @block.sync
                def _(sp):
                    for s in SL:
                        sp.dma_start(bufs[s]["x"][:], tokens(x_in, turn * SLOTS + s)).then_inc(st.sem(f"x_in{s}"), 16)
                    for s in SL:
                        sp.wait_ge(st.sem(f"x_out{s}"), 1)
                        sp.dma_start(tokens(x_out, turn * SLOTS + s), bufs[s]["x"][:]).then_inc(st.sem("stored"), 16)
                    sp.wait_ge(st.sem("stored"), 16 * SLOTS)

                @block.scalar
                def _(act):
                    for s in SL:
                        copy_xT(st, act, f"xT{s}", bufs[s]["xT"])
                    for s in SL:
                        for e in range(HF):
                            act.wait_ge(*st.full(f"gu{s}_{e}"))
                            o = st.region(f"gu{s}_{e}")
                            if e >= 2:
                                act.wait_ge(*st.emptied(f"gu{s}_{e - 2}"))
                            nc.scalar.activation(bufs[s]["silu"][:, e % 2, :], o[:, 0, :], ACT.Silu).then_inc(
                                st.sem(f"silu{s}"), 1)

                @block.vector
                def _(dve):
                    nth = counter()
                    for s in SL:
                        for e in range(HF):
                            dve.wait_ge(*st.full(f"gu{s}_{e}"))
                            o = st.region(f"gu{s}_{e}")
                            dve.wait_ge(st.sem(f"silu{s}"), e + 1)
                            nc.vector.tensor_tensor(bufs[s]["h"][:, e, :], bufs[s]["silu"][:, e % 2, :],
                                                    o[:, 1, :], ALU.mult).then_inc(st.emptying(f"gu{s}_{e}"), 1)
                    for s in SL:
                        Z = bufs[s]
                        dve.wait_ge(*st.full(f"down{s}"))
                        o = st.region(f"down{s}")
                        nc.vector.tensor_tensor(flat(Z["x"][:]), flat(Z["x"][:]), flat(o[:]), ALU.add).then_inc(
                            st.emptying(f"down{s}"), 1)
                        dve.wait_ge(*st.emptied(f"down{s}"))
                        Z["norm"].vector(dve, nth, Z["x"], Z["x"], f"x_out{s}")

                @block.gpsimd
                def _(pool):
                    nth = counter()
                    for s in SL:
                        bufs[s]["norm"].gpsimd(pool, nth, K["neg_half"], 1e-5)
            st.zero_sems()
class Weights:

    def __init__(self, nc, room, arrived, names, shapes):
        self.arrays, self.arrived, at = {}, arrived, 0
        for name in names:
            rows, cols = shapes[name]
            c = -(-rows // P)
            self.arrays[name] = room[:, at:at + c * cols].rearrange("p (c n) -> p c n", c=c)
            at += c * cols
        assert at <= room.shape[1], (at, room.shape)
        self.expected = 0

    def __getitem__(self, name):
        return self.arrays[name]

    def load(self, sp, A):
        for name, dst in self.arrays.items():
            src = A[name]
            if src.shape[0] < P:
                dst = dst[0:src.shape[0], 0, :]
            else:
                src = tiles_of(src)
            if src.dtype == I32:
                dst = dst.bitcast(I32)
            sp.dma_start(dst, src).then_inc(self.arrived, 16)
            self.expected += 16

    def arrive(self, eng):
        eng.wait_ge(self.arrived, self.expected)


LAYERS = [
    ("gla", ("Wq", "Wk", "Wv", "Wg", "Wo", "Wgk1", "Wgk2", "W1", "W2")),
    ("xattn", ("xwq", "xwk", "xwv", "xwo")),
    ("moe", ("gate", "egate", "eup", "edown")),
    ("mamba", ("in_proj", "out_proj")),
    ("psi", ("pWq", "pWo")),
    ("ffn", ("w_gate", "w_up", "w_down")),
]


def build(nc, A, out, run=6):
    with ExitStack() as ctx:
        def sb(name, shape, dt=F32):
            return ctx.enter_context(nc.sbuf_tensor(name, [P] + shape, dt))

        psum = [ctx.enter_context(nc.psum_tensor(f"region{r}", [P, 2, 512], F32)) for r in range(REGIONS + 1)]
        rooms = [sb("weights_even", [9300]), sb("weights_odd", [4608])]
        arrived = [ctx.enter_context(nc.semaphore(f"weights_in{i}")) for i in range(len(LAYERS))]
        consts_in = ctx.enter_context(nc.semaphore("consts_in"))
        made = ctx.enter_context(nc.semaphore("consts_made"))
        cleared = ctx.enter_context(nc.semaphore("psum_cleared"))
        shapes = {n: a.shape for n, a in A.items()}
        weights = [Weights(nc, rooms[i % 2], arrived[i], names, shapes) for i, (_, names) in enumerate(LAYERS)]

        K = {"ident": sb("ident", [P]), "tri": sb("tri", [P]), "ones": sb("ones", [P]),
             "chunk_mask": sb("chunk_mask", [T]), "neg_half": sb("neg_half", [16]), "eps6": sb("eps6", [1])}
        K["sems"] = {"keep": ctx}
        columns = ("ln1_w", "ln1_b", "ln2_w", "ln2_b", "bgk2", "b1", "xwq_b", "xwk_b", "norm_w", "conv_b", "pWq_b")
        col = sb("columns", [sum(shapes[n][0] // P for n in columns)])
        at, loads = 0, []
        for n in columns:
            c = shapes[n][0] // P
            K[n] = col[:, at:at + c]
            loads.append((K[n], A[n].rearrange("(c p) -> p c", p=P)))
            at += c
        spread = ("b2", "xwv_b", "xwo_b", "pWo_b", "dt_bias", "A_log", "geo_w", "temperature")
        row = sb("rows", [sum(shapes[n][0] for n in spread)])
        at = 0
        for n in spread:
            K[n] = row[:, at:at + shapes[n][0]]
            loads.append((K[n], A[n].rearrange("(a n) -> a n", a=1).broadcast_to([P, shapes[n][0]])))
            at += shapes[n][0]
        K["rms_w"], K["mD"], K["conv_w"] = sb("rms_w", [1]), sb("mD", [MF]), sb("conv_w", [MF, 4])
        loads.append((K["conv_w"][:], tiles_of(A["conv_w"])))
        for r in range(2):
            loads.append((K["rms_w"][64 * r:64 * r + 64, :], A["rms_w"].rearrange("(p a) -> p a", a=1)))
            loads.append((K["mD"][64 * r:64 * r + 64, :],
                          A["mD"].rearrange("(f r) -> r f", r=2)[r:r + 1, :].broadcast_to([64, MF])))

        with nc.Block() as block:
            @block.sync
            def _(sp):
                with nc.allow_non_contiguous_dma("small arrays, once"):
                    for dst, src in loads:
                        sp.dma_start(dst, src).then_inc(consts_in, 16)
                weights[0].load(sp, A)
                sp.wait_ge(consts_in, 16 * len(loads))

            @block.gpsimd
            def _(pool):
                count = [0]

                def step(ins):
                    count[0] += 1
                    ins.then_inc(made, 1)
                    pool.wait_ge(made, count[0])

                G = nc.gpsimd
                step(G.memset(K["ident"][:], 0.0))
                step(G.affine_select(out=K["ident"][:], in_=K["ident"][:], compare_op=ALU.not_equal, fill=1.0, base=0,
                                     pattern=[[-1, P]], channel_multiplier=1))
                step(G.memset(K["tri"][:], 1.0))
                step(G.affine_select(out=K["tri"][:], in_=K["tri"][:], compare_op=ALU.is_ge, fill=0.0, base=0,
                                     pattern=[[1, P]], channel_multiplier=-1))
                step(G.memset(K["neg_half"][:], -0.5))
                step(G.memset(K["ones"][:], 1.0))
                step(G.memset(K["eps6"][:], 1e-6))
                step(G.memset(K["chunk_mask"][:], 1.0))
                step(G.memset(K["chunk_mask"][:].rearrange("p (t n) -> p t n", n=P)[:, :, 0:1], 0.0))

            @block.vector
            def _(dve):
                for r in range(REGIONS + 1):
                    nc.vector.memset(psum[r][:], 0.0).then_inc(cleared, 1)
                dve.wait_ge(cleared, REGIONS + 1)

        between = [nc.dram_tensor(f"x_after_{LAYERS[i][0]}", (B, T, D), F32, kind="Internal").ap()
                   for i in range(run - 1)] + [out]
        makers = {"gla": gla_layer, "xattn": xattn_layer, "moe": moe_layer, "mamba": mamba_layer, "psi": psi_layer,
                  "ffn": ffn_layer}
        x = A["x"]
        for i in range(run):
            if i + 1 < run:
                with nc.Block() as block:
                    @block.sync
                    def _(sp):
                        weights[i + 1].load(sp, A)
            makers[LAYERS[i][0]](nc, A, K, psum, x, between[i], weights[i], SLOTS_OF[LAYERS[i][0]])
            x = between[i]


SLOTS_OF = {"gla": 2, "xattn": 1, "moe": 2, "mamba": 1, "psi": 1, "ffn": 2}


def kernel(**inputs):
    import numpy as np
    import concourse.bacc as bacc
    from concourse.bass_utils import run_bass_kernel_spmd as run

    def of(name):
        return np.asarray(inputs[name])

    def t(name):
        return of(name).T

    a = {"x": of("x"), "ctx": of("ctx_1024"), "ctxT": of("ctx_1024").transpose(0, 2, 1)}
    for n in ("ln1_w", "ln1_b", "Wq", "Wk", "Wv", "Wg", "Wgk1", "Wgk2", "bgk2", "rms_w", "Wo", "ln2_w", "ln2_b",
              "W1", "b1", "W2", "b2"):
        a[n] = of("L0_attn_" + n)
    for n in "qkvo":
        a[f"xw{n}"], a[f"xw{n}_b"] = t(f"L0_xattn_w{n}_w"), of(f"L0_xattn_w{n}_b")
    a["gate"] = t("L0_ffn_gate_w")
    a["egate"] = np.concatenate([of("L0_ffn_dyn_gate_w").reshape(NE * P, D), of("L0_ffn_sh_gate_w")[0]]).T
    a["eup"] = np.concatenate([of("L0_ffn_dyn_up_w").reshape(NE * P, D), of("L0_ffn_sh_up_w")[0]]).T
    a["edown"] = np.concatenate([of("L0_ffn_dyn_down_w").transpose(0, 2, 1).reshape(NE * P, D),
                                 of("L0_ffn_sh_down_w")[0].T])
    a["in_proj"], a["out_proj"] = t("L1_attn_in_proj_w"), t("L1_attn_out_proj_w")
    for n in ("norm_w", "conv_w", "conv_b", "A_log", "dt_bias"):
        a[n] = of("L1_attn_" + n)
    a["mD"] = of("L1_attn_D")
    a["pWq"], a["pWq_b"], a["pWo"], a["pWo_b"] = (t("L1_xattn_Wq_w"), of("L1_xattn_Wq_b"), t("L1_xattn_Wo_w"),
                                                   of("L1_xattn_Wo_b"))
    a["proj_w"], a["proj_b"], a["geo_w"] = t("L1_xattn_proj_w"), of("L1_xattn_proj_b"), of("L1_xattn_geo_w")
    a["temperature"] = of("L1_xattn_temperature").reshape(1)
    a["w_gate"], a["w_up"], a["w_down"] = t("L1_ffn_w_gate"), t("L1_ffn_w_up"), t("L1_ffn_w_down")

    nc = bacc.Bacc("TRN2", target_bir_lowering=False, num_devices=1)
    arrays = {"in_" + n: np.ascontiguousarray(v) for n, v in a.items()}
    A = {n[3:]: nc.dram_tensor(n, v.shape, mybir.dt.from_np(v.dtype), kind="ExternalInput").ap()
         for n, v in arrays.items()}
    out = nc.dram_tensor("out", (B, T, D), F32, kind="ExternalOutput").ap()
    build(nc, A, out)
    return run(nc, [arrays], core_ids=[0]).results[0]["out"]
```
